# Optimizing a Trainium2 kernel written in Bass

```python
import numpy as np
import jax
import jax.numpy as jnp

def _softmax(x, axis=-1):
    return jax.nn.softmax(x, axis=axis)

def _gelu(x):
    return jax.nn.gelu(x, approximate=True)

def _silu(x):
    return jax.nn.silu(x)

def _sigmoid(x):
    return jax.nn.sigmoid(x)

def _layernorm(x, axis=-1, eps=1e-05):
    m = jnp.mean(x, axis=axis, keepdims=True)
    v = jnp.var(x, axis=axis, keepdims=True)
    return (x - m) / jnp.sqrt(v + eps)

def _scatter_add(tgt, idx, src, axis=0):
    return tgt.at[idx].add(src)

def _segment_sum(src, seg, n):
    return jax.ops.segment_sum(src, seg, n)
kernel_name = 'mk_gnn_resnorm_d1_gnn_r64_507f1e'

def setup_inputs(seed: int=0):
    np.random.seed(seed)
    _w = jnp.asarray

    def _rec_inputs():
        import jax
        import jax.numpy as jnp
        _gk = jax.random.key(seed)
        x = -0.0003713 + 1 * jax.random.normal(jax.random.fold_in(_gk, 1), (50000, 256), jnp.float32)
        src = jax.random.randint(jax.random.fold_in(_gk, 2), (12500,), 0, 50000, jnp.int32)
        dst = jnp.minimum((50000 * jax.random.uniform(jax.random.fold_in(_gk, 3), (12500,)) ** 2.0).astype(jnp.int32), 49999)
        _o = jnp.argsort(dst, stable=True)
        src = src[_o]
        dst = dst[_o]
        edge_type_8 = jax.random.randint(jax.random.fold_in(_gk, 12), (12500,), 0, 8, jnp.int32)
        return (x, src, dst, edge_type_8)
    x, src, dst, edge_type_8 = _rec_inputs()

    def _L0_gnn_setup():
        import jax, jax.numpy as jnp
        import numpy as np
        N_NODES = 50000
        N_EDGES = 12500
        IN_FEAT = 256
        OUT_FEAT = 256
        NUM_RELS = 8
        ALPHA = 0.5
        key = jax.random.key(seed)
        k1, k2, k3, k4, k5, k6 = jax.random.split(key, 6)
        x = jax.random.normal(k1, (N_NODES, IN_FEAT), dtype=jnp.float32)
        edge_index = jax.random.randint(k2, (2, N_EDGES), 0, N_NODES, dtype=jnp.int64)
        edge_type = jax.random.randint(k3, (N_EDGES,), 0, NUM_RELS, dtype=jnp.int64)
        gain = float(np.sqrt(2.0))
        lim_w = gain * float(np.sqrt(6.0 / (IN_FEAT + OUT_FEAT)))
        weight = jax.random.uniform(k4, (NUM_RELS, IN_FEAT, OUT_FEAT), dtype=jnp.float32, minval=-lim_w, maxval=lim_w)
        loop_weight = jax.random.uniform(k5, (IN_FEAT, OUT_FEAT), dtype=jnp.float32, minval=-lim_w, maxval=lim_w)
        h_bias = jnp.zeros((OUT_FEAT,), dtype=jnp.float32)
        return {'edge_index': edge_index, 'x': x, 'edge_type': edge_type, 'weight': weight, 'h_bias': h_bias, 'loop_weight': loop_weight}
    _L0_gnn_all = _L0_gnn_setup()
    _L0_gnn_in = {k: v for k, v in _L0_gnn_all.items() if k in ('weight', 'h_bias', 'loop_weight')}
    del _L0_gnn_all
    return {'x': x, 'src': src, 'dst': dst, 'edge_type_8': edge_type_8, 'L0_gnn_weight': _L0_gnn_in['weight'], 'L0_gnn_h_bias': _L0_gnn_in['h_bias'], 'L0_gnn_loop_weight': _L0_gnn_in['loop_weight']}

def reference(x, src, dst, edge_type_8, L0_gnn_weight, L0_gnn_h_bias, L0_gnn_loop_weight):
    import jax
    import jax.numpy as jnp

    def _L0_gnn_ref(edge_index, x, edge_type, weight, h_bias, loop_weight):
        import jax, jax.numpy as jnp
        import numpy as np
        N_NODES = 50000
        N_EDGES = 12500
        IN_FEAT = 256
        OUT_FEAT = 256
        NUM_RELS = 8
        ALPHA = 0.5
        num_nodes = x.shape[0]
        src, dst = (edge_index[0], edge_index[1])
        hx = jnp.einsum('ni,rio->rno', x, weight)
        msg = hx[edge_type, src]
        agg = jax.ops.segment_sum(msg, dst, num_segments=num_nodes)
        node_repr = agg * jnp.asarray(ALPHA, x.dtype) ** 0.5
        node_repr = node_repr + h_bias
        loop_message = x @ loop_weight
        node_repr = node_repr + loop_message * jnp.asarray(1.0 - ALPHA, x.dtype) ** 0.5
        return node_repr
    edge_index = jnp.stack([src, dst])
    x = _layernorm(x + _L0_gnn_ref(edge_index, x, edge_type_8, L0_gnn_weight, L0_gnn_h_bias, L0_gnn_loop_weight), axis=-1)
    return x

_drawn_inputs = setup_inputs


def setup_inputs(seed=0):
    import zlib

    import numpy as np

    out = dict(_drawn_inputs(seed))
    spreads = {'L0_gnn_h_bias': (0.0, 0.1)}
    factors = {}
    for name, (base, spread) in spreads.items():
        noise = np.random.default_rng([zlib.crc32(name.encode()), seed]).standard_normal(out[name].shape)
        drawn = base * np.exp(spread * noise) if base else spread * noise
        out[name] = jnp.asarray(drawn.astype(out[name].dtype))
    for name, factor in factors.items():
        out[name] = (out[name] * factor).astype(out[name].dtype)
    return out
```

```python
from contextlib import ExitStack

import numpy as np

import concourse.bass as bass
from concourse import mybir

ALU = mybir.AluOpType
ACT = mybir.ActivationFunctionType
F32 = mybir.dt.float32
F32R = mybir.dt.float32r
I32 = mybir.dt.int32
AX_X = mybir.AxisListType.X

P = 128
SKIP = 1 << 20
EPS = 1e-5
RUN = P - 1

XT_RING = 2
Y_RING = 4
BLOCK_RING = 4
PERM_RING = 8


class Phase:

    def __init__(self, kinds, n, before):
        self.kinds, self.n, self.size = kinds, n, len(kinds)
        self.before = dict(before)

    def after(self):
        return {k: v + self.n * self.kinds.count(k) for k, v in self.before.items()}


class Pair:

    def __init__(self, phases, at, s, j):
        self.phases, self.at, self.s, self.j = phases, at, s, j
        self.phase = phases[at]
        self.kind = self.phase.kinds[j]
        self.looped = not isinstance(s, int)

    def count(self, kinds):
        ph = self.phase
        fixed = sum(ph.before[k] + ph.kinds[:self.j].count(k) for k in kinds)
        per = sum(ph.kinds.count(k) for k in kinds)
        return self.s * per + fixed

    def fixed(self, kinds):
        ph = self.phase
        mine = sum(ph.before[k] + ph.kinds[:self.j].count(k) for k in kinds)
        return mine if self.looped else mine + self.s * sum(ph.kinds.count(k) for k in kinds)

    def turns(self, kinds, ring):
        ph = self.phase
        per = sum(ph.kinds.count(k) for k in kinds)
        if self.looped:
            assert per % ring == 0, (ph.kinds, kinds, ring)
            return self.s * (per // ring) + self.fixed(kinds) // ring
        return self.fixed(kinds) // ring

    def ahead(self, d):
        if self.looped:
            k = self.j + d
            step, j = k // self.phase.size, k % self.phase.size
            return Pair(self.phases, self.at, self.s + step if step else self.s, j)
        at, k = self.at, self.s * self.phase.size + self.j + d
        while k < 0:
            at -= 1
            if at < 0:
                return None
            k += self.phases[at].n * self.phases[at].size
        while k >= self.phases[at].n * self.phases[at].size:
            k -= self.phases[at].n * self.phases[at].size
            at += 1
            if at == len(self.phases):
                return None
        return Pair(self.phases, at, k // self.phases[at].size, k % self.phases[at].size)


def walk(eng, phases, step):
    for at, ph in enumerate(phases):
        peel = ph.n < 4

        def once(s):
            for j in range(ph.size):
                step(Pair(phases, at, s, j))

        if peel:
            for s in range(ph.n):
                once(s)
            continue
        once(0)
        with eng.Fori(1, ph.n - 1) as s:
            once(s)
        once(ph.n - 1)


def past(eng, sem):
    eng.sem_inc(sem, 1)


def wait(eng, sem, value):
    if isinstance(value, int) and value <= 0:
        return
    eng.wait_ge(sem, value)


def gnn_layernorm_kernel(nc, x, src, dst, rel, weight, bias, loop_weight, out):
    N, D = x.shape
    E = src.shape[0]
    R = weight.shape[0]
    KT = D // P
    C = float(np.float32(0.5) ** np.float32(0.5))

    EC = -(-E // P)
    EROWS, EREST = E // EC, E % EC
    MT = (E + R * (P - 1)) // P
    MPAIRS = -(-MT // 2)
    MTP = 2 * MPAIRS
    FT = -(-E // RUN)
    FPAIRS = -(-FT // 2)
    FTP = 2 * FPAIRS

    BROWS = 4 * P
    BLOCKS = N // BROWS
    LEFT = N - BLOCKS * BROWS
    assert 2 * P < LEFT < 3 * P and KT == 2 and FTP * RUN >= E
    REST = LEFT - 2 * P
    MAIN = 2 * BLOCKS + 2

    first = 4
    mix = MPAIRS // 4
    mix_rest = MPAIRS - 4 * mix
    last = (MAIN - 8 * first - 8 * mix - 2 * mix_rest) // 8
    last_rest = MAIN - 8 * first - 8 * mix - 2 * mix_rest - 8 * last
    phases, before = [], {"m": 0, "g": 0, "f": 0}
    for kinds, n in (("m" * 8, first), ("gmm" * 4, mix), ("gmm" * mix_rest, 1), ("f" * 8, FPAIRS // 8),
                     ("f" * (FPAIRS % 8), 1), ("m" * 8, last), ("m" * last_rest, 1)):
        if kinds:
            phases.append(Phase(kinds, n, before))
            before = phases[-1].after()
    assert before == {"m": MAIN, "g": MPAIRS, "f": FPAIRS}
    PAIRS = sum(before.values())
    SORT_PER = 4
    SORTED = 8 * SORT_PER * (first - 1)
    assert SORTED <= EC <= SORTED + PERM_RING

    UNIT = 8
    UNITS = -(-FTP // UNIT)
    KEYS = 1 + UNITS * UNIT * RUN + 1
    MROWS = FTP * RUN + 1
    message_rows = nc.dram_tensor("message_rows", (MROWS, D), F32).ap()
    padded_dst = nc.dram_tensor("padded_dst", (KEYS,), I32).ap()

    with ExitStack() as ctx:
        def sb(name, shape, dt):
            return ctx.enter_context(nc.sbuf_tensor(name, shape, dt))

        def sem(name):
            return ctx.enter_context(nc.semaphore(name))

        fixed_rows = sb("fixed_rows", [P, FTP * D], F32)
        W_AT = FTP * D - R * KT * D
        w_rel = fixed_rows[:, W_AT:]
        w_main = sb("w_main", [P, KT * D], F32)
        w_high = sb("w_high", [P, KT * D], F32R)
        w_low = sb("w_low", [P, KT * D], F32R)
        x_in = sb("x_in", [P, BLOCK_RING, 4, D], F32)
        y_out = sb("y_out", [P, BLOCK_RING, 4, D], F32)
        xt_high = sb("xt_high", [P, Y_RING, 2 * D], F32R)
        xt_low = sb("xt_low", [P, Y_RING, 2 * D], F32R)
        xt_full = sb("xt_full", [P, Y_RING, 2 * D], F32)
        gathered = sb("gathered", [P, 4, D], F32)
        message_out = sb("message_out", [P, 4, D], F32)
        message_in = sb("message_in", [P, 8, D], F32)
        keys = sb("keys", [P, 2, UNIT * RUN], I32)
        same = sb("same", [P, 4, P], F32)
        ident = sb("ident", [P, P], F32)
        bias_b = sb("bias_b", [P, D], F32)
        src_at = sb("src_at", [P, MTP], I32)
        edge_at = sb("edge_at", [P, MTP], I32)
        fix_at = sb("fix_at", [P, FTP], I32)
        src_stage = sb("src_stage", [P, 8], I32)
        edge_stage = sb("edge_stage", [P, 8], I32)
        fix_stage = sb("fix_stage", [P, 16], I32)
        row_key = sb("row_key", [P, FTP], F32)
        w_offset = sb("w_offset", [1, MTP], I32)
        stats = sb("stats", [P, 4, 4, 6], F32)
        mean_var = sb("mean_var", [P, 4, 4, 2], F32)
        std = sb("std", [P, 4, 4], F32)
        rstd = sb("rstd", [P, 4, 4], F32)
        shift = sb("shift", [P, 4, 4], F32)
        eps = sb("eps", [P, 1], F32)
        minus = sb("minus", [P, 8], I32)

        at = [0]

        def scratch(n, dt=F32):
            a = fixed_rows[:, at[0]:at[0] + n]
            at[0] += n
            assert at[0] <= W_AT
            return a if dt == F32 else a.bitcast(dt)

        rel_i, src_i, pos_i, hi_i, lo_i, e1_i = (scratch(EC, I32) for _ in range(6))
        rel_f, src_f, pos_f, hi_f, lo_f, e1_f, edge1, live = (scratch(EC) for _ in range(8))
        onehot, running, placed = (scratch(R * EC) for _ in range(3))
        count, total, prior, tiles_f, incl, start, offset, tot_f = (scratch(R) for _ in range(8))
        tot_i, tiles_i, riota_i = (scratch(R, I32) for _ in range(3))
        riota = scratch(R)
        iota_i = scratch(P, I32)
        iota_f = scratch(P)
        upper, ones = scratch(P), scratch(P)
        rel_ge = scratch(MTP * (R - 1))
        rel_n = scratch(MTP)
        pick = scratch(PERM_RING * (P + 2 * MTP))
        pick = pick.rearrange("p (r n) -> p r n", r=PERM_RING)
        key_i, next_i = scratch(P, I32), scratch(P, I32)
        key_f, next_f, key_eq, key_at = (scratch(P) for _ in range(4))
        e1_back, e1_zero = scratch(MTP), scratch(MTP)
        loop_raw = scratch(KT * D)
        zero = scratch(2 * D)

        xt_ps = [ctx.enter_context(nc.psum_tensor(f"xt_ps{i}", [P, 2 * D], F32)) for i in range(XT_RING)]
        y_ps = [ctx.enter_context(nc.psum_tensor(f"y_ps{i}", [P, 2 * D], F32)) for i in range(Y_RING)]
        perm_ps = ctx.enter_context(nc.psum_tensor("perm_ps", [P, 512], F32))
        misc_ps = ctx.enter_context(nc.psum_tensor("misc_ps", [P, 512], F32))

        weights_in = sem("weights_in")
        edges_in = sem("edges_in")
        pads_out = sem("pads_out")
        keys_in = sem("keys_in")
        pool_consts = sem("pool_consts")
        dve_consts = sem("dve_consts")
        dve_step = sem("dve_step")
        counts_ready = sem("counts_ready")
        counts_summed = sem("counts_summed")
        picks_built = sem("picks_built")
        picks_used = sem("picks_used")
        lists_ready = sem("lists_ready")
        keys_ready = sem("keys_ready")
        keys_turned = sem("keys_turned")
        fix_lists_ready = sem("fix_lists_ready")
        w_ready = sem("w_ready")
        x_loaded = [sem(f"x_loaded{i}") for i in range(BLOCK_RING)]
        x_rest_loaded = sem("x_rest_loaded")
        rows_gathered = [sem(f"rows_gathered{i}") for i in range(2)]
        turned = sem("turned")
        copied = sem("copied")
        low_done = sem("low_done")
        product = sem("product")
        tile_sum = sem("tile_sum")
        moved = sem("moved")
        message_moved = sem("message_moved")
        stats_done = sem("stats_done")
        moments = sem("moments")
        std_ready = sem("std_ready")
        rstd_ready = sem("rstd_ready")
        scale_ready = sem("scale_ready")
        normed = sem("normed")
        stored = [sem(f"stored{i}") for i in range(BLOCK_RING)]
        scattered = [sem(f"scattered{i}") for i in range(2)]
        staged = sem("staged")
        pool_past = sem("pool_past")
        dve_past = sem("dve_past")
        corner_zero = sem("corner_zero")
        message_loaded = [sem(f"message_loaded{i}") for i in range(4)]
        keys_loaded = [sem(f"keys_loaded{i}") for i in range(2)]
        same_built = sem("same_built")
        carried = sem("carried")
        rest_stored = sem("rest_stored")
        fixes_out = sem("fixes_out")

        def block_rows(table, b):
            return table[bass.ds(b * BROWS, BROWS), :].rearrange("(p t) d -> p t d", t=4)

        def ln_group(p):
            n = p.fixed("mf")
            return p.turns("mf", 2), (n // 2) % 4, n % 2

        def y_tile(p, t):
            if p.kind == "f":
                return fixed_rows[:, bass.ds(p.count("f") * (2 * D) + t * D, D)]
            m = p.fixed("m")
            return y_out[:, (m // 2) % BLOCK_RING, 2 * (m % 2) + t, :]

        def has_carry(p, t):
            return t == 0 or (p.ahead(1) is not None and p.ahead(1).kind == "f")

        def sort_columns(p):
            if p.at != 0:
                return []
            if not p.looped and p.s == first - 1:
                return [(c, c % PERM_RING) for c in range(SORTED, EC)] if p.j == 0 else []
            return [(p.s * (8 * SORT_PER) + SORT_PER * p.j + i, (SORT_PER * p.j + i) % PERM_RING) for i in range(SORT_PER)]

        def sort_ends(p):
            return not p.looped and p.at == 0 and p.s == first - 1 and p.j == 0

        def product_tile(p, t):
            q = p.fixed("mgf")
            if p.kind == "f":
                return y_ps[(q + 2 * t) % Y_RING][:, 0:D]
            return y_ps[q % Y_RING][:, t * D:(t + 1) * D]

        block = ctx.enter_context(nc.Block())

        @block.sync
        def _(sp):
            sp.wait_ge(dve_consts, 3)
            for tile, table in ((rel_i, rel), (src_i, src)):
                sp.dma_start(tile[0:EROWS, :], table[0:EROWS * EC].rearrange("(p c) -> p c", c=EC)).then_inc(edges_in, 16)
                sp.dma_start(tile[EROWS:EROWS + 1, 0:EREST],
                             table[EROWS * EC:E].rearrange("(p c) -> p c", p=1)).then_inc(edges_in, 16)

            def load_block(b, slot):
                if isinstance(b, int) and b == BLOCKS:
                    sp.dma_start(x_in[:, slot, 0:2, :], x[b * BROWS:b * BROWS + 2 * P, :].rearrange("(p t) d -> p t d", t=2)).then_inc(x_loaded[slot], 16)
                    sp.dma_start(x_in[0:REST, slot, 2, :], x[N - REST:N, :]).then_inc(x_rest_loaded, 16)
                elif not isinstance(b, int) or b < BLOCKS:
                    sp.dma_start(x_in[:, slot, :, :], block_rows(x, b)).then_inc(x_loaded[slot], 16)

            for b in range(2):
                load_block(b, b)
            sp.dma_start(loop_raw.rearrange("p (k n) -> p k n", k=KT), loop_weight.rearrange("(k p) n -> p k n", p=P)).then_inc(weights_in, 16)
            sp.dma_start(bias_b[:, :], bias.partition_broadcast(P)).then_inc(weights_in, 16)
            for b in range(2, BLOCK_RING):
                load_block(b, b)
            sp.dma_start(w_rel.rearrange("p (r k n) -> p r k n", r=R, k=KT), weight.rearrange("r (k p) n -> p r k n", p=P)).then_inc(weights_in, 16)
            sp.dma_start(padded_dst[1:E + 1].rearrange("(a b) -> a b", b=100), dst.rearrange("(a b) -> a b", b=100)).then_inc(pads_out, 16)
            sp.wait_ge(pool_consts, 2)
            sp.dma_start(padded_dst[0:1].rearrange("(a b) -> a b", a=1), minus[0:1, 0:1]).then_inc(pads_out, 16)
            tail = KEYS - (E + 1)
            whole = tail // 8 * 8
            sp.dma_start(padded_dst[E + 1:E + 1 + whole].rearrange("(a b) -> a b", b=8), minus[0:whole // 8, :]).then_inc(pads_out, 16)
            if tail > whole:
                sp.dma_start(padded_dst[E + 1 + whole:KEYS].rearrange("(a b) -> a b", a=1), minus[0:1, 0:tail - whole]).then_inc(pads_out, 16)
            sp.dma_start(message_rows[0:1, :], zero[0:1, 0:D]).then_inc(pads_out, 16)
            pads = MROWS - (E + 1)
            assert pads % 2 == 0 and pads // 2 <= P
            sp.dma_start(message_rows[E + 1:MROWS, :].rearrange("(p t) d -> p (t d)", t=2), zero[0:pads // 2, :]).then_inc(pads_out, 16)
            sp.wait_ge(pads_out, 16 * (5 + (tail > whole)))
            windows = bass.AP(tensor=padded_dst.tensor, offset=0, ap=[[RUN, FTP], [1, P]])
            after = bass.AP(tensor=padded_dst.tensor, offset=1, ap=[[RUN, FTP], [1, P]])
            sp.dma_start(key_i[0:FTP, :], windows).then_inc(keys_in, 16)
            sp.dma_start(next_i[0:FTP, :], after).then_inc(keys_in, 16)

            def load_keys(u, slot):
                sp.dma_start(keys[:, slot, :], padded_dst[bass.ds(u * (UNIT * RUN) + 1, UNIT * RUN)].partition_broadcast(P)).then_inc(keys_loaded[slot], 16)

            for u in range(2):
                load_keys(u, u)

            def load_messages(i, slot):
                for t in range(2):
                    sp.dma_start(message_in[:, 2 * slot + t, :], message_rows[bass.ds((i + t) * RUN, P), :]).then_inc(message_loaded[slot], 16)

            def step(p):
                if p.kind == "f":
                    slot = p.fixed("f") % 4
                    following = p.count("f") + 4
                    if p.looped or following < FPAIRS:
                        sp.wait_ge(product, p.count("mgf") + 1)
                        load_messages(following * 2, slot)
                    if slot == 3:
                        unit = p.turns("f", 4)
                        uslot = (p.fixed("f") // 4) % 2
                        if p.looped or unit + 2 < UNITS:
                            sp.wait_ge(same_built, (unit + 1) * UNIT)
                            load_keys(unit + 2, uslot)
                after_p = p.ahead(1)
                if after_p is not None and after_p.kind == "f" and p.kind != "f":
                    for i in range(2):
                        sp.wait_ge(scattered[i], 32 * ((MPAIRS + 1 - i) // 2))
                    for f in range(min(4, FPAIRS)):
                        load_messages(2 * f, f)
                if p.kind != "m" or p.fixed("m") % 2 == 0:
                    return
                b, slot = p.turns("m", 2), (p.fixed("m") // 2) % BLOCK_RING
                if p.looped or b + 4 <= BLOCKS:
                    sp.wait_ge(turned, p.count("mgf") + 1)
                    load_block(b + 4, slot)
                sp.wait_ge(normed, p.count("mf") + 1)
                if isinstance(b, int) and b == BLOCKS:
                    sp.dma_start(out[b * BROWS:b * BROWS + 2 * P, :].rearrange("(p t) d -> p t d", t=2), y_out[:, slot, 0:2, :]).then_inc(stored[slot], 16)
                    sp.dma_start(out[N - REST:N, :], y_out[0:REST, slot, 2, :]).then_inc(rest_stored, 16)
                else:
                    sp.dma_start(block_rows(out, b), y_out[:, slot, :, :]).then_inc(stored[slot], 16)

            walk(sp, phases, step)
            sp.wait_ge(fixes_out, 16 * FTP)

        @block.gpsimd
        def _(pool):
            nc.gpsimd.memset(minus[:, :], -1).then_inc(pool_consts, 1)
            nc.gpsimd.memset(zero[:, :], 0.0).then_inc(pool_consts, 1)
            nc.gpsimd.memset(ones[:, :], 1.0).then_inc(pool_consts, 1)
            nc.gpsimd.memset(ident[:, :], 0.0).then_inc(pool_consts, 1)
            nc.gpsimd.memset(eps[:, :], EPS).then_inc(pool_consts, 1)
            nc.gpsimd.iota(riota_i[:, :], [[1, R]], base=0, channel_multiplier=0).then_inc(pool_consts, 1)
            nc.gpsimd.iota(iota_i[:, :], [[1, P]], base=0, channel_multiplier=0).then_inc(pool_consts, 1)
            nc.gpsimd.iota(e1_i[:, :], [[1, EC]], base=1, channel_multiplier=EC).then_inc(pool_consts, 1)
            pool.wait_ge(pool_consts, 8)
            nc.gpsimd.affine_select(out=ident[:, :], in_=ident[:, :], compare_op=ALU.not_equal, fill=1.0, base=0,
                                    pattern=[[-1, P]], channel_multiplier=1).then_inc(pool_consts, 1)
            nc.gpsimd.affine_select(out=upper[:, :], in_=ones[:, :], compare_op=ALU.is_gt, fill=0.0, base=0,
                                    pattern=[[1, P]], channel_multiplier=-1).then_inc(pool_consts, 1)
            nc.gpsimd.memset(gathered[:, :, :], 0.0).then_inc(corner_zero, 1)

            def gather(at_list, column, slot, t):
                nc.gpsimd.indirect_dma_start(gathered[:, 2 * slot + t, :], None, x,
                                             bass.IndirectOffsetOnAxis(ap=at_list[:, column:column + 1], axis=0),
                                             bounds_check=N - 1, oob_is_err=False).then_inc(rows_gathered[slot], 16)

            pool.wait_ge(corner_zero, 1)
            pool.wait_ge(lists_ready, 2)
            for c in range(4):
                gather(src_at, c, c // 2, c % 2)

            def slot_uses(p, kinds, i, lead, total):
                n = sum(p.phase.before[k] for k in kinds) + lead
                per = sum(p.phase.kinds.count(k) for k in kinds)
                if p.looped:
                    return p.s * (per // 2) + (n + 1 - i) // 2
                return (min(n + p.s * per, total) + 1 - i) // 2

            def stage(p, kind, per, tiles, lists):
                base = p.s * per + p.phase.before[kind] * 2
                n = 0
                for to, of, lead in lists:
                    width = min(to.shape[1], tiles - (p.phase.before[kind] * 2 + p.s * per + lead)) if not p.looped else to.shape[1]
                    if width > 0:
                        nc.gpsimd.tensor_copy(to[:, 0:width], of[:, bass.ds(base + lead, width)]).then_inc(staged, 1)
                        n += 1
                return n

            def step(p):
                if p.kind == "m":
                    return
                if p.kind == "g":
                    slot = p.fixed("g") % 2
                    width = 2 * p.phase.kinds.count("g")
                    if p.j == 0:
                        for i in range(2):
                            wait(pool, rows_gathered[i], 32 * slot_uses(p, "g", i, 2, MPAIRS))
                            wait(pool, scattered[i], 32 * slot_uses(p, "g", i, 0, MPAIRS))
                        past(pool, pool_past)
                        stage(p, "g", width, MTP, ((src_stage[:, 0:width], src_at, 4), (edge_stage[:, 0:width], edge_at, 0)))
                        nc.gpsimd.drain()
                    column = 2 * (p.phase.kinds[:p.j].count("g"))
                    if p.looped or p.count("g") + 2 < MPAIRS:
                        pool.wait_ge(turned, p.count("mgf") + 1)
                        past(pool, pool_past)
                        for t in range(2):
                            gather(src_stage, column + t, slot, t)
                    pool.wait_ge(message_moved, p.count("g") + 1)
                    past(pool, pool_past)
                    for t in range(2):
                        nc.gpsimd.indirect_dma_start(message_rows, bass.IndirectOffsetOnAxis(ap=edge_stage[:, column + t:column + t + 1], axis=0),
                                                     message_out[:, 2 * slot + t, :], None,
                                                     bounds_check=MROWS - 1, oob_is_err=False).then_inc(scattered[slot], 16)
                    if not p.looped and p.count("g") == MPAIRS - 1:
                        pool.wait_ge(turned, p.count("mgf") + 1)
                        nc.gpsimd.memset(gathered[0:1, :, :], 0.0).then_inc(corner_zero, 1)
                        pool.wait_ge(corner_zero, 2)
                        pool.wait_ge(fix_lists_ready, 1)
                        for c in range(4):
                            gather(fix_at, c, (MPAIRS + c // 2) % 2, c % 2)
                    return
                slot = (MPAIRS + p.fixed("f")) % 2
                width = 2 * p.phase.size
                if p.j == 0:
                    for i in range(2):
                        wait(pool, rows_gathered[i], 32 * slot_uses(p, "gf", i, 2, MPAIRS + FPAIRS))
                    past(pool, pool_past)
                    stage(p, "f", width, FTP, ((fix_stage[:, 0:width], fix_at, 4),))
                    nc.gpsimd.drain()
                if p.looped or p.count("f") + 2 < FPAIRS:
                    pool.wait_ge(turned, p.count("mgf") + 1)
                    past(pool, pool_past)
                    for t in range(2):
                        gather(fix_stage, 2 * p.j + t, slot, t)

            walk(pool, phases, step)
            for i in range(BLOCK_RING):
                pool.wait_ge(stored[i], 16 * ((BLOCKS + BLOCK_RING - i) // BLOCK_RING))
            pool.wait_ge(normed, MAIN + FPAIRS)
            pool.wait_ge(rest_stored, 16)
            for i in range(FTP):
                nc.gpsimd.indirect_dma_start(out, bass.IndirectOffsetOnAxis(ap=fix_at[:, i:i + 1], axis=0),
                                             fixed_rows[:, i * D:(i + 1) * D], None,
                                             bounds_check=N - 1, oob_is_err=False).then_inc(fixes_out, 16)
            pool.wait_ge(fixes_out, 16 * FTP)

        @block.vector
        def _(dve):
            steps = [0]

            def link(ins):
                steps[0] += 1
                ins.then_inc(dve_step, 1)
                dve.wait_ge(dve_step, steps[0])

            nc.vector.memset(rel_i[:, :], R).then_inc(dve_consts, 1)
            nc.vector.memset(src_i[:, :], 0).then_inc(dve_consts, 1)
            nc.vector.memset(prior[:, :], 0.0).then_inc(dve_consts, 1)
            dve.wait_ge(pool_consts, 10)
            dve.wait_ge(dve_consts, 3)
            link(nc.vector.tensor_copy(riota[:, :], riota_i[:, :]))
            link(nc.vector.tensor_copy(iota_f[:, :], iota_i[:, :]))
            link(nc.vector.tensor_copy(e1_f[:, :], e1_i[:, :]))
            link(nc.vector.tensor_scalar(live[:, :], e1_f[:, :], E + 0.5, None, ALU.is_lt))
            link(nc.vector.tensor_tensor(edge1[:, :], e1_f[:, :], live[:, :], ALU.mult))
            dve.wait_ge(edges_in, 64)
            link(nc.vector.tensor_copy(rel_f[:, :], rel_i[:, :]))
            link(nc.vector.tensor_copy(src_f[:, :], src_i[:, :]))
            oh = onehot.rearrange("p (r c) -> p r c", r=R)
            rn = running.rearrange("p (r c) -> p r c", r=R)
            pl = placed.rearrange("p (r c) -> p r c", r=R)
            link(nc.vector.tensor_tensor(oh, rel_f.unsqueeze(1).broadcast_to([P, R, EC]), riota.unsqueeze(2).broadcast_to([P, R, EC]), ALU.is_equal))
            nc.vector.tensor_reduce(count[:, :], oh, AX_X, ALU.add).then_inc(counts_ready, 1)
            link(nc.vector.tensor_tensor_scan(running[:, :], onehot[:, :], onehot[:, :], 0.0, ALU.add, ALU.max))
            link(nc.vector.tensor_copy(prior[:, 1:R], rn[:, 0:R - 1, EC - 1]))
            dve.wait_ge(counts_summed, 1)
            link(nc.vector.tensor_copy(total[:, :], misc_ps[:, R:2 * R]))
            link(nc.vector.tensor_scalar(tot_f[:, :], total[:, :], float(P - 1), None, ALU.add))
            link(nc.vector.tensor_copy(tot_i[:, :], tot_f[:, :]))
            link(nc.vector.tensor_scalar(tiles_i[:, :], tot_i[:, :], 7, None, ALU.logical_shift_right))
            link(nc.vector.tensor_copy(tiles_f[:, :], tiles_i[:, :]))
            link(nc.vector.tensor_tensor_scan(incl[:, :], tiles_f[:, :], tiles_f[:, :], 0.0, ALU.add, ALU.max))
            link(nc.vector.tensor_tensor(start[:, :], incl[:, :], tiles_f[:, :], ALU.subtract))
            link(nc.vector.scalar_tensor_tensor(out=offset[:, :], in0=start[:, :], scalar=float(P), in1=prior[:, :], op0=ALU.mult, op1=ALU.subtract))
            link(nc.vector.scalar_tensor_tensor(out=count[:, :], in0=offset[:, :], scalar=-1.0, in1=misc_ps[:, 0:R], op0=ALU.add, op1=ALU.add))
            link(nc.vector.tensor_tensor(pl, rn, count.unsqueeze(2).broadcast_to([P, R, EC]), ALU.add))
            link(nc.vector.tensor_tensor(rn, pl, oh, ALU.mult))
            link(nc.vector.tensor_reduce(pos_f[:, :], running.rearrange("p (r c) -> p c r", r=R), AX_X, ALU.add))
            link(nc.vector.tensor_copy(pos_i[:, :], pos_f[:, :]))
            link(nc.vector.tensor_scalar(hi_i[:, :], pos_i[:, :], 7, None, ALU.logical_shift_right))
            link(nc.vector.tensor_scalar(lo_i[:, :], pos_i[:, :], P - 1, None, ALU.bitwise_and))
            link(nc.vector.tensor_copy(hi_f[:, :], hi_i[:, :]))
            link(nc.vector.tensor_copy(lo_f[:, :], lo_i[:, :]))
            ge = rel_ge[0:1, :].rearrange("p (k r) -> p k r", r=R - 1)
            link(nc.vector.tensor_tensor(ge, iota_f[0:1, 0:MTP].unsqueeze(2).broadcast_to([1, MTP, R - 1]),
                                         start[0:1, 1:R].unsqueeze(1).broadcast_to([1, MTP, R - 1]), ALU.is_ge))
            link(nc.vector.tensor_reduce(rel_n[0:1, :], ge, AX_X, ALU.add))
            link(nc.vector.tensor_scalar(w_offset[:, :], rel_n[0:1, :], float(KT * D), float(W_AT), ALU.mult, ALU.add))
            dve.wait_ge(weights_in, 48)
            link(nc.vector.tensor_scalar(w_main[:, :], loop_raw[:, :], C, None, ALU.mult))
            for k in range(KT):
                d = w_main[:, k * D + k * P:k * D + k * P + P]
                link(nc.vector.tensor_tensor(d, d, ident[:, :], ALU.add))
            link(nc.vector.tensor_copy(w_high[:, :], w_main[:, :]))
            nc.vector.tensor_tensor(w_low[:, :], w_main[:, :], w_high[:, :].bitcast(F32), ALU.subtract).then_inc(w_ready, 1)

            dve.wait_ge(keys_in, 32)
            link(nc.vector.tensor_copy(key_f[0:FTP, :], key_i[0:FTP, :]))
            link(nc.vector.tensor_copy(next_f[0:FTP, :], next_i[0:FTP, :]))
            link(nc.vector.tensor_tensor(key_eq[0:FTP, :], key_f[0:FTP, :], next_f[0:FTP, :], ALU.is_equal))
            link(nc.vector.scalar_tensor_tensor(out=key_at[0:FTP, :], in0=key_eq[0:FTP, :], scalar=float(SKIP), in1=key_f[0:FTP, :], op0=ALU.mult, op1=ALU.add))
            nc.vector.memset(key_at[0:FTP, 0:1], float(SKIP)).then_inc(keys_ready, 1)
            dve.wait_ge(keys_turned, 1)
            nc.vector.tensor_copy(row_key[:, :], misc_ps[:, 128:128 + FTP]).then_inc(fix_lists_ready, 0 + 1)
            nc.vector.tensor_copy(fix_at[:, :], misc_ps[:, 256:256 + FTP]).then_inc(fix_lists_ready, 1)
            dve.wait_ge(fix_lists_ready, 2)

            def low(p):
                if p is None or p.kind != "m":
                    return
                slot = p.fixed("mgf") % Y_RING
                dve.wait_ge(copied, p.count("mgf") + 1)
                nc.vector.tensor_tensor(xt_low[:, slot, :], xt_ps[slot % XT_RING][:, :], xt_high[:, slot, :].bitcast(F32), ALU.subtract).then_inc(low_done, 1)

            def same_keys(p):
                if p is None or p.kind != "f":
                    return
                slot, unit_slot = p.fixed("f") % 4, (p.fixed("f") // 4) % 2
                if slot == 0:
                    dve.wait_ge(keys_loaded[unit_slot], 16 * (p.turns("f", 8) + 1))
                wait(dve, product, p.count("mgf") - 1)
                for t in range(2):
                    key = row_key[:, bass.ds(p.count("f") * 2 + t, 1)]
                    k0 = (2 * slot + t) * RUN
                    to = same[:, 2 * (slot % 2) + t, :]
                    nc.vector.tensor_scalar(to[:, 1:P], keys[:, unit_slot, k0:k0 + RUN], key, None, ALU.is_equal).then_inc(same_built, 0 + 1)
                    nc.vector.tensor_scalar(to[:, 0:1], keys[:, unit_slot, k0 + RUN - 1:k0 + RUN], key, None, ALU.is_equal).then_inc(same_built, 1)

            def coefficients(p):
                if p is None or p.kind == "g":
                    return
                g, slot, half = ln_group(p)
                if half == 0:
                    return
                dve.wait_ge(std_ready, g + 1)
                wait(dve, normed, (g - 3) * 2)
                nc.vector.reciprocal(rstd[:, slot, :], std[:, slot, :]).then_inc(rstd_ready, 1)
                dve.wait_ge(rstd_ready, g + 1)
                nc.vector.scalar_tensor_tensor(out=shift[:, slot, :], in0=mean_var[:, slot, :, 0], scalar=-1.0, in1=rstd[:, slot, :],
                                               op0=ALU.mult, op1=ALU.mult).then_inc(scale_ready, 1)

            first_pair = Pair(phases, 0, 0, 0)
            low(first_pair)
            low(first_pair.ahead(1))

            def step(p):
                low(p.ahead(2))
                for c, slot in sort_columns(p):
                    wait(dve, picks_used, c - PERM_RING + 1)
                    lo, hi = lo_f[:, bass.ds(c, 1)], hi_f[:, bass.ds(c, 1)]
                    nc.vector.tensor_scalar(pick[:, slot, 0:P], iota_f[:, :], lo, None, ALU.is_equal)
                    nc.vector.tensor_scalar(pick[:, slot, P:P + MTP], iota_f[:, 0:MTP], hi, src_f[:, bass.ds(c, 1)], ALU.is_equal, ALU.mult)
                    nc.vector.tensor_scalar(pick[:, slot, P + MTP:], iota_f[:, 0:MTP], hi, edge1[:, bass.ds(c, 1)], ALU.is_equal, ALU.mult).then_inc(picks_built, 1)
                same_keys(p.ahead(1))
                if p.kind != "g":
                    g, slot, half = ln_group(p)
                    q = p.fixed("mgf") % Y_RING
                    dve.wait_ge(product, p.count("mgf") + 1)
                    if p.kind == "m" and half == 0:
                        m = p.fixed("m") // 2
                        wait(dve, stored[m % BLOCK_RING], 16 * p.turns("m", 2 * BLOCK_RING))
                    bias_2 = bias_b[:, :].unsqueeze(1).broadcast_to([P, 2, D])
                    if p.kind == "m":
                        m = p.fixed("m")
                        to = y_out[:, (m // 2) % BLOCK_RING, 2 * (m % 2):2 * (m % 2) + 2, :]
                        nc.vector.tensor_tensor(to, y_ps[q][:, :].rearrange("p (t d) -> p t d", t=2), bias_2, ALU.add).then_inc(moved, 1)
                    else:
                        for t in range(2):
                            if has_carry(p, t):
                                dve.wait_ge(carried, p.count("f") * 2 + t + 1)
                            last = nc.vector.tensor_tensor(y_tile(p, t), product_tile(p, t), bias_b[:, :], ALU.add)
                        last.then_inc(moved, 1)
                if p.ahead(-1) is not None:
                    coefficients(p.ahead(-1))
                if p.kind != "g":
                    n = p.count("mf")
                    dve.wait_ge(moved, n + 1)
                    past(dve, dve_past)
                    for t in range(2):
                        nc.vector.bn_stats(stats[:, slot, 2 * half + t, :], y_tile(p, t)).then_inc(stats_done, 1)
                    for t in range(2):
                        dve.wait_ge(stats_done, n * 2 + t + 1)
                        past(dve, dve_past)
                        nc.vector.bn_aggr(mean_var[:, slot, 2 * half + t, :], stats[:, slot, 2 * half + t, :]).then_inc(moments, 1)
                if sort_ends(p):
                    dve.wait_ge(picks_used, EC + 1)
                    nc.vector.tensor_copy(src_at[:, :], perm_ps[:, 0:MTP]).then_inc(lists_ready, 1)
                    link(nc.vector.tensor_copy(e1_back[:, :], perm_ps[:, MTP:2 * MTP]))
                    link(nc.vector.tensor_scalar(e1_zero[:, :], e1_back[:, :], 0.0, None, ALU.is_equal))
                    nc.vector.scalar_tensor_tensor(out=edge_at[:, :], in0=e1_zero[:, :], scalar=float(SKIP), in1=e1_back[:, :],
                                                   op0=ALU.mult, op1=ALU.add).then_inc(lists_ready, 1)

            walk(dve, phases, step)
            end = Pair(phases, len(phases) - 1, phases[-1].n - 1, phases[-1].size - 1)
            coefficients(end)

        @block.scalar
        def _(act):
            def copy_xt(p):
                if p is None:
                    return
                n, slot = p.count("mgf"), p.fixed("mgf") % Y_RING
                act.wait_ge(turned, n + 1)
                wait(act, product, n - Y_RING + 1)
                to = xt_high if p.kind == "m" else xt_full
                nc.scalar.activation(to[:, slot, :], xt_ps[slot % XT_RING][:, :], ACT.Copy).then_inc(copied, 1)

            def carry(p, t):
                if p is None or p.kind != "f":
                    return
                if not has_carry(p, t):
                    return
                nxt = p if t == 0 else p.ahead(1)
                slot = nxt.fixed("f") % 4
                act.wait_ge(message_loaded[slot], 32 * (nxt.turns("f", 4) + 1))
                if t == 0:
                    act.wait_ge(tile_sum, p.count("f") + 1)
                else:
                    act.wait_ge(product, p.count("mgf") + 1)
                nc.scalar.activation(message_in[0:1, 2 * slot + 1 - t, :], product_tile(p, t)[0:1, :], ACT.Copy).then_inc(carried, 1)

            def move_message(p):
                if p is None or p.kind != "g":
                    return
                q, slot = p.fixed("mgf") % Y_RING, p.fixed("g") % 2
                act.wait_ge(product, p.count("mgf") + 1)
                wait(act, scattered[slot], 32 * p.turns("g", 2))
                nc.scalar.activation(message_out[:, 2 * slot:2 * slot + 2, :], y_ps[q][:, :].rearrange("p (t d) -> p t d", t=2),
                                     ACT.Copy, scale=C).then_inc(message_moved, 1)

            def deviation(p):
                if p is None or p.kind == "g":
                    return
                g, slot, half = ln_group(p)
                if half == 0:
                    return
                act.wait_ge(moments, (g + 1) * 4)
                nc.scalar.activation(std[:, slot, :], mean_var[:, slot, :, 1], ACT.Sqrt, bias=eps[:, 0:1]).then_inc(std_ready, 1)

            def norm(p, t):
                if p.kind == "g":
                    return
                g, slot, half = ln_group(p)
                if t == 0:
                    act.wait_ge(scale_ready, g + 1)
                i = 2 * half + t
                a = nc.scalar.activation(y_tile(p, t), y_tile(p, t), ACT.Identity, scale=rstd[:, slot, i:i + 1], bias=shift[:, slot, i:i + 1])
                if t == 1:
                    a.then_inc(normed, 1)

            act.wait_ge(pool_consts, 10)
            first_pair = Pair(phases, 0, 0, 0)
            for d in range(5):
                copy_xt(first_pair.ahead(d))
                if d >= 3:
                    deviation(first_pair.ahead(d - 3))

            def step(p):
                copy_xt(p.ahead(5))
                carry(p.ahead(3), 0)
                norm(p, 0)
                carry(p.ahead(3), 1)
                move_message(p.ahead(3))
                deviation(p.ahead(2))
                norm(p, 1)

            walk(act, phases, step)

        @block.tensor
        def _(pe):
            def turn(p):
                if p is None:
                    return
                n, q = p.count("mgf"), p.fixed("mgf")
                if p.kind == "m":
                    m = p.fixed("m")
                    slot = (m // 2) % BLOCK_RING
                    if m % 2 == 0:
                        pe.wait_ge(x_loaded[slot], 16 * (p.turns("m", 2 * BLOCK_RING) + 1))
                    elif not p.looped and p.count("m") == MAIN - 1:
                        pe.wait_ge(x_rest_loaded, 16)
                    rows = [x_in[:, slot, 2 * (m % 2) + t, :] for t in range(2)]
                else:
                    gf = p.fixed("gf")
                    pe.wait_ge(rows_gathered[gf % 2], 32 * (p.turns("gf", 2) + 1))
                    rows = [gathered[:, 2 * (gf % 2) + t, :] for t in range(2)]
                before = p.ahead(-1)
                if before is not None:
                    wait(pe, copied, n - 1)
                    wait(pe, low_done, before.count("m"))
                for t in range(2):
                    for k in range(KT):
                        last = nc.tensor.transpose(xt_ps[q % XT_RING][:, t * D + k * P:t * D + (k + 1) * P], rows[t][:, k * P:(k + 1) * P], ident[:, :])
                last.then_inc(turned, 1)

            def multiply(p, offsets):
                n, q = p.count("mgf"), p.fixed("mgf") % Y_RING
                pe.wait_ge(copied, n + 1)
                if p.kind == "m":
                    pe.wait_ge(low_done, p.count("m") + 1)
                for d in (Y_RING, 2):
                    user = p.ahead(-d)
                    if user is None or (d == 2 and "f" not in (p.kind, user.kind)):
                        continue
                    if user.kind == "g":
                        pe.wait_ge(message_moved, user.count("g") + 1)
                    else:
                        pe.wait_ge(moved, user.count("mf") + 1)
                for t in range(2):
                    to = product_tile(p, t)

                    def part(xt, w, k, start, stop):
                        return nc.tensor.matmul(to, xt[:, q, t * D + k * P:t * D + (k + 1) * P], w, start=start, stop=stop)

                    for k in range(KT):
                        ws = slice(k * D, (k + 1) * D)
                        end = k == KT - 1
                        if p.kind == "m":
                            part(xt_high, w_low[:, ws], k, k == 0, False)
                            part(xt_low, w_high[:, ws], k, False, False)
                            last = part(xt_high, w_high[:, ws], k, False, end)
                        elif p.kind == "g":
                            last = part(xt_full, fixed_rows[:, bass.ds(offsets[t] + k * D, D)], k, k == 0, end)
                        else:
                            part(xt_full, w_main[:, ws], k, k == 0, False)
                    if p.kind == "f":
                        f = p.count("f")
                        slot = p.fixed("f") % 4
                        if t == 0:
                            pe.wait_ge(message_loaded[slot], 32 * (p.turns("f", 4) + 1))
                            pe.wait_ge(same_built, f * 4 + 4)
                        wait(pe, carried, f * 2 + t)
                        last = nc.tensor.matmul(to, same[:, 2 * (slot % 2) + t, :], message_in[:, 2 * slot + t, :], start=False, stop=True)
                        if t == 0:
                            last.then_inc(tile_sum, 1)
                last.then_inc(product, 1)

            pe.wait_ge(pool_consts, 10)
            pe.wait_ge(counts_ready, 1)
            nc.tensor.matmul(misc_ps[:, 0:R], upper[:, :], count[:, :], start=True, stop=True)
            nc.tensor.matmul(misc_ps[:, R:2 * R], ones[:, :], count[:, :], start=True, stop=True).then_inc(counts_summed, 1)
            pe.wait_ge(keys_ready, 1)
            nc.tensor.transpose(misc_ps[:, 128:128 + FTP], key_f[0:FTP, :], ident[0:FTP, 0:FTP])
            nc.tensor.transpose(misc_ps[:, 256:256 + FTP], key_at[0:FTP, :], ident[0:FTP, 0:FTP]).then_inc(keys_turned, 1)
            nc.tensor.matmul(perm_ps[:, 0:2 * MTP], zero[:, 0:P], zero[:, 0:2 * MTP], start=True, stop=False)

            first_pair = Pair(phases, 0, 0, 0)
            turn(first_pair)
            turn(first_pair.ahead(1))
            pe.wait_ge(w_ready, 1)

            def step(p):
                offsets = None
                if p.kind == "g":
                    n = p.count("g") * 2
                    offsets = [pe.value_load(w_offset[0:1, bass.ds(n + t, 1)], min_val=W_AT, max_val=W_AT + (R - 1) * KT * D) for t in range(2)]
                turn(p.ahead(2))
                multiply(p, offsets)
                for c, slot in sort_columns(p):
                    pe.wait_ge(picks_built, c + 1)
                    nc.tensor.matmul(perm_ps[:, 0:2 * MTP], pick[:, slot, 0:P], pick[:, slot, P:], start=False, stop=False).then_inc(picks_used, 1)
                if sort_ends(p):
                    nc.tensor.matmul(perm_ps[:, 0:2 * MTP], zero[:, 0:P], zero[:, 0:2 * MTP], start=False, stop=True).then_inc(picks_used, 1)

            walk(pe, phases, step)


_INS = ["x", "src", "dst", "edge_type_8", "L0_gnn_weight", "L0_gnn_h_bias", "L0_gnn_loop_weight"]


def kernel(**inputs):
    import concourse.bacc as bacc
    from concourse.bass_utils import run_bass_kernel_spmd

    nc = bacc.Bacc("TRN2", target_bir_lowering=False, num_devices=1)
    arrays, args = {}, []
    for name in _INS:
        a = np.ascontiguousarray(inputs[name])
        arrays[f"in_{name}"] = a
        args.append(nc.dram_tensor(f"in_{name}", a.shape, mybir.dt.from_np(a.dtype), kind="ExternalInput").ap())
    args.append(nc.dram_tensor("out_rows", inputs["x"].shape, F32, kind="ExternalOutput").ap())
    gnn_layernorm_kernel(nc, *args)
    r = run_bass_kernel_spmd(nc, [arrays], core_ids=[0])
    return r.results[0]["out_rows"]
```

```python
from contextlib import ExitStack

import numpy as np

import concourse.bass as bass
from concourse import mybir

ALU = mybir.AluOpType
ACT = mybir.ActivationFunctionType
F32 = mybir.dt.float32
F32R = mybir.dt.float32r
I32 = mybir.dt.int32
AX_X = mybir.AxisListType.X

P = 128
SKIP = 1 << 20
EPS = 1e-5
RUN = P - 1

XT_RING = 2
Y_RING = 4
BLOCK_RING = 4
LATE = 2
ROWS_RING = 4
FIX_RING = 8
FIRST = 8
MORE = 2
PLAIN = (0, 3, 6)
SPLIT_FIX = (2, 6, 10, 14)
TAIL = 4


class Phase:

    def __init__(self, kinds, n, plain, before):
        self.kinds, self.n, self.size = kinds, n, len(kinds)
        self.split = [j not in plain for j in range(self.size)]
        self.before = dict(before)

    def after(self):
        after = {k: v + self.n * self.kinds.count(k) for k, v in self.before.items()}
        after["split"] = self.before["split"] + self.n * sum(self.split)
        return after


class Pair:

    def __init__(self, phases, at, s, j):
        self.phases, self.at, self.s, self.j = phases, at, s, j
        self.phase = phases[at]
        self.kind = self.phase.kinds[j]
        self.looped = not isinstance(s, int)
        self.plain = not self.phase.split[j]

    def count(self, kinds):
        ph = self.phase
        fixed = sum(ph.before[k] + ph.kinds[:self.j].count(k) for k in kinds)
        per = sum(ph.kinds.count(k) for k in kinds)
        return self.s * per + fixed

    def splits(self):
        return self.phase.before["split"] + self.s * sum(self.phase.split) + sum(self.phase.split[:self.j])

    def fixed(self, kinds):
        ph = self.phase
        mine = sum(ph.before[k] + ph.kinds[:self.j].count(k) for k in kinds)
        return mine if self.looped else mine + self.s * sum(ph.kinds.count(k) for k in kinds)

    def turns(self, kinds, ring):
        ph = self.phase
        per = sum(ph.kinds.count(k) for k in kinds)
        if self.looped:
            assert per % ring == 0, (ph.kinds, kinds, ring)
            return self.s * (per // ring) + self.fixed(kinds) // ring
        return self.fixed(kinds) // ring

    def ahead(self, d):
        if self.looped:
            k = self.j + d
            step, j = k // self.phase.size, k % self.phase.size
            return Pair(self.phases, self.at, self.s + step if step else self.s, j)
        at, k = self.at, self.s * self.phase.size + self.j + d
        while k < 0:
            at -= 1
            if at < 0:
                return None
            k += self.phases[at].n * self.phases[at].size
        while k >= self.phases[at].n * self.phases[at].size:
            k -= self.phases[at].n * self.phases[at].size
            at += 1
            if at == len(self.phases):
                return None
        return Pair(self.phases, at, k // self.phases[at].size, k % self.phases[at].size)


def nth(p, kind, n):
    way = 1 if n > 0 else -1
    d = 0
    while n:
        d += way
        q = p.ahead(d)
        if q is None:
            return None
        if q.kind == kind:
            n -= way
    return q


def walk(eng, phases, step):
    for at, ph in enumerate(phases):
        peel = ph.n < 4

        def once(s):
            for j in range(ph.size):
                step(Pair(phases, at, s, j))

        if peel:
            for s in range(ph.n):
                once(s)
            continue
        once(0)
        with eng.Fori(1, ph.n - 1) as s:
            once(s)
        once(ph.n - 1)


def past(eng, sem):
    eng.sem_inc(sem, 1)


def wait(eng, sem, value):
    if isinstance(value, int) and value <= 0:
        return
    eng.wait_ge(sem, value)


def gnn_layernorm_kernel(nc, x, src, dst, rel, weight, bias, loop_weight, out):
    N, D = x.shape
    E = src.shape[0]
    R = weight.shape[0]
    KT = D // P
    C = float(np.float32(0.5) ** np.float32(0.5))

    EC = -(-E // P)
    EROWS, EREST = E // EC, E % EC
    MT = (E + R * (P - 1)) // P
    MPAIRS = -(-MT // 2)
    MTP = 2 * MPAIRS
    FT = -(-E // RUN)
    FPAIRS = -(-FT // 2)
    FTP = 2 * FPAIRS

    BROWS = 4 * P
    BLOCKS = N // BROWS
    LEFT = N - BLOCKS * BROWS
    assert 2 * P < LEFT < 3 * P and KT == 2 and FTP * RUN >= E
    REST = LEFT - 2 * P
    MAIN = 2 * BLOCKS + 2

    first = FIRST
    turns = MPAIRS // 3 // 2
    assert 3 * turns % 8 == 0
    mix_rest = MPAIRS - 6 * turns
    mixes = (FPAIRS - TAIL) // 8
    fix_rest = FPAIRS - 8 * mixes - TAIL
    pause = MAIN - 8 * first - MORE - 8 * turns - 2 * mix_rest - FPAIRS
    assert pause >= 4
    mix, mix_at = "gmgmgmm" * turns, 2
    mixed, rest = "fm" * 8, "fm" * fix_rest + "m" * TAIL + "f" * TAIL

    def places(kinds, kind):
        return [j for j in range(len(kinds)) if kinds[j] == kind]

    phases, before = [], {"m": 0, "g": 0, "f": 0, "split": 0}
    for kinds, n, plain in (("m" * 8, first, PLAIN),
                            ("m" * MORE, 1, ()),
                            (mix, 1, places(mix, "g")),
                            (mix, 1, ()),
                            ("gmm" * mix_rest, 1, ()),
                            ("m" * pause, 1, ()),
                            (mixed, mixes, [j for j in places(mixed, "f") if j not in SPLIT_FIX]),
                            (rest, 1, places(rest, "f"))):
        if kinds and n:
            phases.append(Phase(kinds, n, plain, before))
            before = phases[-1].after()
    assert (before["m"], before["g"], before["f"]) == (MAIN, MPAIRS, FPAIRS)
    FIX_FROM = MAIN - FPAIRS

    BEHIND = 4
    EARLY = FPAIRS - 3

    def written(fixed_main):
        return fixed_main // 2 - 3

    EARLY_ROW, EARLY_STEP = BROWS * written(FIX_FROM + BEHIND) - 3 * BROWS // 4, BROWS // 4
    assert all(EARLY_ROW + EARLY_STEP * i <= BROWS * written(FIX_FROM + i // 2 + BEHIND) for i in range(2 * EARLY))
    SORT_PER = 7
    assert EC % (2 * SORT_PER) == 0

    WINDOWS = 10
    CHUNKS = FTP // WINDOWS
    assert CHUNKS * WINDOWS == FTP and CHUNKS % 2 == 0 and WINDOWS <= 4 * BLOCK_RING

    UNIT = 8
    UNITS = -(-FTP // UNIT)
    KEYS = 1 + UNITS * UNIT * RUN + 1
    MROWS = FTP * RUN + 1
    grouped = nc.dram_tensor("grouped", (P * MTP, 2), I32).ap()
    message_rows = nc.dram_tensor("message_rows", (MROWS, D), F32).ap()
    padded_dst = nc.dram_tensor("padded_dst", (KEYS,), I32).ap()

    with ExitStack() as ctx:
        def sb(name, shape, dt):
            return ctx.enter_context(nc.sbuf_tensor(name, shape, dt))

        def sem(name):
            return ctx.enter_context(nc.semaphore(name))

        w_rel_high = sb("w_rel_high", [P, R * KT * D], F32R)
        w_rel_low = sb("w_rel_low", [P, R * KT * D], F32R)
        w_rel = sb("w_rel", [P, R * KT * D], F32)
        y_fix = sb("y_fix", [P, FIX_RING, 2, D], F32)
        work = sb("work", [P, 10000], F32)
        w_main = sb("w_main", [P, KT * D], F32)
        w_high = sb("w_high", [P, KT * D], F32R)
        w_low = sb("w_low", [P, KT * D], F32R)
        x_in = sb("x_in", [P, BLOCK_RING, 4, D], F32)
        y_out = sb("y_out", [P, BLOCK_RING, 4, D], F32)
        xt_high = sb("xt_high", [P, Y_RING, 2 * D], F32R)
        xt_low = sb("xt_low", [P, Y_RING, 2 * D], F32R)
        xt_full = sb("xt_full", [P, Y_RING, 2 * D], F32)
        gathered = sb("gathered", [P, 2 * ROWS_RING, D], F32)
        message_out = sb("message_out", [P, 4, D], F32)
        message_in = sb("message_in", [P, 8, D], F32)
        keys = sb("keys", [P, 2, UNIT, P], I32)
        same = sb("same", [P, 8, P], F32)
        ident = sb("ident", [P, P], F32)
        bias_b = sb("bias_b", [P, D], F32)
        list_at = sb("list_at", [P, MTP, 2], I32)
        src_at, edge_at = list_at[:, :, 0], list_at[:, :, 1]
        fix_at = sb("fix_at", [P, FTP], I32)
        src_stage = sb("src_stage", [P, 16], I32)
        edge_stage = sb("edge_stage", [P, 16], I32)
        place_stage = sb("place_stage", [P, 2 * SORT_PER], I32)
        entry_stage = sb("entry_stage", [P, 2 * SORT_PER, 2], I32)
        entries = sb("entries", [P, EC, 2], I32)
        fix_src_stage = sb("fix_src_stage", [P, 16], I32)
        fix_out_stage = sb("fix_out_stage", [P, 16], I32)
        row_key = sb("row_key", [P, FTP], F32)
        w_offset = sb("w_offset", [1, MTP], I32)
        stats = sb("stats", [P, 4, 4, 6], F32)
        mean_var = sb("mean_var", [P, 4, 4, 2], F32)
        std = sb("std", [P, 4, 4], F32)
        rstd = sb("rstd", [P, 4, 4], F32)
        shift = sb("shift", [P, 4, 4], F32)
        eps = sb("eps", [P, 1], F32)
        minus = sb("minus", [P, 8], I32)

        disorder = sb("disorder", [P, 1], F32)
        early_bound = sb("early_bound", [P, 1], F32)
        early_bound_i = sb("early_bound_i", [P, 1], I32)
        repair_flag = sb("repair_flag", [1, 1], I32)
        own_keys = sb("own_keys", [P, P], I32)
        edge_key = sb("edge_key", [P, FTP], F32)
        later = sb("later", [P, P], F32)
        later_n = sb("later_n", [P, 1], F32)
        rows_f = sb("rows_f", [P, 1], F32)
        rows_i = sb("rows_i", [P, 1], I32)

        at = [0]

        def scratch(n, dt=F32):
            a = work[:, at[0]:at[0] + n]
            at[0] += n
            assert at[0] <= work.shape[1]
            return a if dt == F32 else a.bitcast(dt)

        rel_i, src_i, pos_i, hi_i, lo_i, e1_i = (scratch(EC, I32) for _ in range(6))
        rel_f, pos_f, hi_f, lo_f, e1_f, dead, place_f = (scratch(EC) for _ in range(7))
        place_i = scratch(EC, I32)
        onehot, running, placed = (scratch(R * EC) for _ in range(3))
        count, total, prior, tiles_f, incl, start, offset, tot_f = (scratch(R) for _ in range(8))
        tot_i, tiles_i, riota_i = (scratch(R, I32) for _ in range(3))
        riota = scratch(R)
        iota_i = scratch(P, I32)
        iota_f = scratch(P)
        upper, ones = scratch(P), scratch(P)
        rel_ge = scratch(MTP * (R - 1))
        rel_n = scratch(MTP)
        key_i, next_i = scratch(P, I32), scratch(P, I32)
        key_f, next_f, key_eq, key_at = (scratch(P) for _ in range(4))
        blank = scratch(2 * MTP, I32)
        loop_raw = scratch(KT * D)
        zero = scratch(2 * D)

        xt_ps = [ctx.enter_context(nc.psum_tensor(f"xt_ps{i}", [P, 2 * D], F32)) for i in range(XT_RING)]
        y_ps = [ctx.enter_context(nc.psum_tensor(f"y_ps{i}", [P, 2 * D], F32)) for i in range(Y_RING)]
        misc_ps = ctx.enter_context(nc.psum_tensor("misc_ps", [P, 512], F32))

        weights_in = sem("weights_in")
        loop_in = sem("loop_in")
        edges_in = sem("edges_in")
        pads_out = sem("pads_out")
        keys_in = sem("keys_in")
        pool_consts = sem("pool_consts")
        dve_consts = sem("dve_consts")
        dve_step = sem("dve_step")
        counts_ready = sem("counts_ready")
        counts_summed = sem("counts_summed")
        places_ready = sem("places_ready")
        table_blank = sem("table_blank")
        columns_staged = sem("columns_staged")
        columns_written = [sem(f"columns_written{i}") for i in range(2)]
        list_loaded = sem("list_loaded")
        keys_ready = sem("keys_ready")
        keys_turned = sem("keys_turned")
        fix_lists_ready = sem("fix_lists_ready")
        w_ready = sem("w_ready")
        x_loaded = [sem(f"x_loaded{i}") for i in range(BLOCK_RING)]
        x_rest_loaded = sem("x_rest_loaded")
        rows_gathered = [sem(f"rows_gathered{i}") for i in range(ROWS_RING)]
        turned = sem("turned")
        copied = sem("copied")
        low_done = sem("low_done")
        rel_high = sem("rel_high")
        rel_split = sem("rel_split")
        product = sem("product")
        tile_sum = sem("tile_sum")
        moved = sem("moved")
        fix_scattered = [sem(f"fix_scattered{i}") for i in range(FIX_RING)]
        message_moved = sem("message_moved")
        stats_done = sem("stats_done")
        moments = sem("moments")
        std_ready = sem("std_ready")
        rstd_ready = sem("rstd_ready")
        scale_ready = sem("scale_ready")
        normed = sem("normed")
        stored = [sem(f"stored{i}") for i in range(BLOCK_RING)]
        scattered = [sem(f"scattered{i}") for i in range(2)]
        staged = sem("staged")
        pool_past = sem("pool_past")
        dve_past = sem("dve_past")
        sp_past = sem("sp_past")
        act_past = sem("act_past")
        pe_past = sem("pe_past")
        corner_zero = sem("corner_zero")
        message_loaded = [sem(f"message_loaded{i}") for i in range(4)]
        keys_loaded = [sem(f"keys_loaded{i}") for i in range(2)]
        keys_filled = sem("keys_filled")
        same_built = sem("same_built")
        carried = sem("carried")
        rest_stored = sem("rest_stored")
        flag_ready = sem("flag_ready")
        bound_made = sem("bound_made")
        disorder_ready = sem("disorder_ready")
        repair_open = sem("repair_open")
        own_keys_loaded = sem("own_keys_loaded")
        own_keys_used = sem("own_keys_used")
        rows_ready = sem("rows_ready")
        repair_gathered = sem("repair_gathered")
        repair_turned = sem("repair_turned")
        repair_copied = sem("repair_copied")
        repair_product = sem("repair_product")
        repair_var = sem("repair_var")
        repair_std = sem("repair_std")
        repair_scale = sem("repair_scale")
        repair_result = sem("repair_result")
        repair_written = sem("repair_written")
        repair_done = sem("repair_done")
        chunk_loaded = [sem(f"chunk_loaded{i}") for i in range(2)]
        masks_built = sem("masks_built")
        edge_key_ready = sem("edge_key_ready")
        repair_chain = sem("repair_chain")
        chunk_used = sem("chunk_used")

        def block_rows(table, b):
            return table[bass.ds(b * BROWS, BROWS), :].rearrange("(p t) d -> p t d", t=4)

        def ln_group(p):
            n = p.fixed("mf")
            return p.turns("mf", 2), (n // 2) % 4, n % 2

        def y_tile(p, t):
            if p.kind == "f":
                return y_fix[:, p.fixed("f") % FIX_RING, t, :]
            m = p.fixed("m")
            return y_out[:, (m // 2) % BLOCK_RING, 2 * (m % 2) + t, :]

        def has_carry(p, t):
            return t == 0 or nth(p, "f", 1) is not None

        def sort_step(p):
            return p.j if p.at == 0 and not p.looped and p.s == 0 else None

        def list_step(p):
            return p.j if p.at == mix_at and not p.looped and p.s == 0 else None

        PART = R * KT * D // 8

        def split_part(p, s):
            n = p.phase.kinds[:p.j].count("g") - s
            return PART * n if p.at == mix_at and p.kind == "g" and 0 <= n < 8 else None

        def product_tile(p, t):
            q = p.fixed("mgf")
            if p.kind == "f":
                return y_ps[(q + 2 * t) % Y_RING][:, 0:D]
            return y_ps[q % Y_RING][:, t * D:(t + 1) * D]

        message_chunk = [buffer[:, :, :, :].rearrange("p b t d -> p (b t) d") for buffer in (x_in, y_out)]
        masks = [w_rel[:, b * WINDOWS * P:(b + 1) * WINDOWS * P].rearrange("p (j m) -> p j m", m=P) for b in range(2)]
        repair_y = y_fix[:, 0, 0, :]

        def needs_repair(eng):
            eng.wait_ge(flag_ready, 1)
            return eng.value_load(repair_flag[0:1, 0:1], min_val=0, max_val=1 << 20) > 0

        block = ctx.enter_context(nc.Block())

        @block.sync
        def _(sp):
            sp.wait_ge(dve_consts, 3)
            for tile, table in ((rel_i, rel), (src_i, src)):
                sp.dma_start(tile[0:EROWS, :], table[0:EROWS * EC].rearrange("(p c) -> p c", c=EC)).then_inc(edges_in, 16)
                sp.dma_start(tile[EROWS:EROWS + 1, 0:EREST],
                             table[EROWS * EC:E].rearrange("(p c) -> p c", p=1)).then_inc(edges_in, 16)

            def load_block(b, slot):
                if isinstance(b, int) and b == BLOCKS:
                    sp.dma_start(x_in[:, slot, 0:2, :], x[b * BROWS:b * BROWS + 2 * P, :].rearrange("(p t) d -> p t d", t=2)).then_inc(x_loaded[slot], 16)
                    sp.dma_start(x_in[0:REST, slot, 2, :], x[N - REST:N, :]).then_inc(x_rest_loaded, 16)
                elif not isinstance(b, int) or b < BLOCKS:
                    sp.dma_start(x_in[:, slot, :, :], block_rows(x, b)).then_inc(x_loaded[slot], 16)

            load_block(0, 0)
            sp.dma_start(loop_raw.rearrange("p (k n) -> p k n", k=KT), loop_weight.rearrange("(k p) n -> p k n", p=P)).then_inc(loop_in, 16)
            sp.dma_start(bias_b[:, :], bias.partition_broadcast(P)).then_inc(weights_in, 16)
            for b in range(1, BLOCK_RING):
                load_block(b, b)
            sp.dma_start(w_rel[:, :].rearrange("p (r k n) -> p r k n", r=R, k=KT), weight.rearrange("r (k p) n -> p r k n", p=P)).then_inc(weights_in, 16)
            sp.dma_start(padded_dst[1:E + 1].rearrange("(a b) -> a b", b=100), dst.rearrange("(a b) -> a b", b=100)).then_inc(pads_out, 16)
            sp.wait_ge(pool_consts, 4)
            sp.dma_start(grouped.rearrange("(p k) n -> p (k n)", p=P), blank[:, :]).then_inc(table_blank, 16)
            sp.dma_start(padded_dst[0:1].rearrange("(a b) -> a b", a=1), minus[0:1, 0:1]).then_inc(pads_out, 16)
            tail = KEYS - (E + 1)
            whole = tail // 8 * 8
            sp.dma_start(padded_dst[E + 1:E + 1 + whole].rearrange("(a b) -> a b", b=8), minus[0:whole // 8, :]).then_inc(pads_out, 16)
            if tail > whole:
                sp.dma_start(padded_dst[E + 1 + whole:KEYS].rearrange("(a b) -> a b", a=1), minus[0:1, 0:tail - whole]).then_inc(pads_out, 16)
            sp.dma_start(message_rows[0:1, :], zero[0:1, 0:D]).then_inc(pads_out, 16)
            pads = MROWS - (E + 1)
            assert pads % 2 == 0 and pads // 2 <= P
            sp.dma_start(message_rows[E + 1:MROWS, :].rearrange("(p t) d -> p (t d)", t=2), zero[0:pads // 2, :]).then_inc(pads_out, 16)
            sp.wait_ge(pads_out, 16 * (5 + (tail > whole)))
            windows = bass.AP(tensor=padded_dst.tensor, offset=0, ap=[[RUN, FTP], [1, P]])
            after = bass.AP(tensor=padded_dst.tensor, offset=1, ap=[[RUN, FTP], [1, P]])
            sp.dma_start(key_i[0:FTP, :], windows).then_inc(keys_in, 16)
            sp.dma_start(next_i[0:FTP, :], after).then_inc(keys_in, 16)

            def load_keys(u, slot):
                sp.dma_start(keys[:, slot, :, 1:P], padded_dst[bass.ds(u * (UNIT * RUN) + 1, UNIT * RUN)].rearrange("(t k) -> t k", k=RUN).partition_broadcast(P)).then_inc(keys_loaded[slot], 16)

            for u in range(2):
                load_keys(u, u)

            def load_messages(i, slot):
                for t in range(2):
                    sp.dma_start(message_in[:, 2 * slot + t, :], message_rows[bass.ds((i + t) * RUN, P), :]).then_inc(message_loaded[slot], 16)

            def step(p):
                if p.kind == "f":
                    slot = p.fixed("f") % 4
                    following = p.count("f") + 4
                    if p.looped or following < FPAIRS:
                        sp.wait_ge(product, p.count("mgf") + 1)
                        load_messages(following * 2, slot)
                    if slot == 3:
                        unit = p.turns("f", 4)
                        uslot = (p.fixed("f") // 4) % 2
                        if p.looped or unit + 2 < UNITS:
                            sp.wait_ge(same_built, (unit + 1) * UNIT)
                            load_keys(unit + 2, uslot)
                after_p = p.ahead(5)
                if not p.looped and after_p is not None and after_p.kind == "f" and after_p.count("f") == 0:
                    for i in range(2):
                        sp.wait_ge(scattered[i], 32 * ((MPAIRS + 1 - i) // 2))
                    for f in range(min(4, FPAIRS)):
                        load_messages(2 * f, f)
                if p.kind != "m" or p.fixed("m") % 2 == 0:
                    return
                b, slot = p.turns("m", 2), (p.fixed("m") // 2) % BLOCK_RING
                if p.looped or b + 4 <= BLOCKS:
                    sp.wait_ge(turned, p.count("mgf") + 1)
                    load_block(b + 4, slot)
                if p.looped or b >= LATE:
                    store_block(b - LATE, (slot - LATE) % BLOCK_RING, nth(p, "m", -2 * LATE))

            def store_block(b, slot, ends):
                sp.wait_ge(normed, ends.count("mf") + 1)
                if isinstance(b, int) and b == BLOCKS:
                    sp.dma_start(out[b * BROWS:b * BROWS + 2 * P, :].rearrange("(p t) d -> p t d", t=2), y_out[:, slot, 0:2, :]).then_inc(stored[slot], 16)
                    sp.dma_start(out[N - REST:N, :], y_out[0:REST, slot, 2, :]).then_inc(rest_stored, 16)
                else:
                    sp.dma_start(block_rows(out, b), y_out[:, slot, :, :]).then_inc(stored[slot], 16)

            walk(sp, phases, step)
            end = Pair(phases, len(phases) - 1, 0, phases[-1].size - 1)
            for b in range(BLOCKS + 1 - LATE, BLOCKS + 1):
                store_block(b, b % BLOCK_RING, nth(end, "m", 2 * (b - BLOCKS) - 1))
            sp.wait_ge(rest_stored, 16)
            for i in range(BLOCK_RING):
                sp.wait_ge(stored[i], 16 * ((BLOCKS + BLOCK_RING - i) // BLOCK_RING))

            message_windows = bass.AP(tensor=message_rows.tensor, offset=0, ap=[[RUN * D, FTP], [D, P], [1, D]])
            with sp.If(needs_repair(sp)):
                sp.wait_ge(repair_open, 1)
                with sp.Fori(0, FTP) as i:
                    sp.wait_ge(own_keys_used, i + 1)
                    past(sp, sp_past)
                    sp.dma_start(own_keys[:, :], padded_dst[bass.ds(i * RUN, P)].partition_broadcast(P)).then_inc(own_keys_loaded, 16)
                    with sp.Fori(0, CHUNKS // 2) as c:
                        for half in range(2):
                            sp.wait_ge(chunk_used, i * CHUNKS + c * 2 + half + 1)
                            past(sp, sp_past)
                            sp.dma_start(message_chunk[half][:, 0:WINDOWS, :],
                                         message_windows[bass.ds((c * 2 + half) * WINDOWS, WINDOWS), :, :].rearrange("j p d -> p j d")).then_inc(chunk_loaded[half], 16)

        @block.gpsimd
        def _(pool):
            nc.gpsimd.memset(minus[:, :], -1).then_inc(pool_consts, 1)
            nc.gpsimd.memset(zero[:, :], 0.0).then_inc(pool_consts, 1)
            nc.gpsimd.iota(early_bound_i[:, :], [[0, 1]], base=EARLY_ROW, channel_multiplier=EARLY_STEP).then_inc(bound_made, 1)
            pool.wait_ge(bound_made, 1)
            nc.gpsimd.tensor_copy(early_bound[:, :], early_bound_i[:, :]).then_inc(bound_made, 1)
            pool.wait_ge(bound_made, 2)
            nc.gpsimd.affine_select(out=early_bound[:, :], in_=early_bound[:, :], compare_op=ALU.is_gt, fill=float(SKIP), base=2 * EARLY,
                                    pattern=[[0, 1]], channel_multiplier=-1).then_inc(bound_made, 1)
            nc.gpsimd.memset(blank.rearrange("p (k n) -> p k n", n=2)[:, :, 0], 0).then_inc(pool_consts, 1)
            nc.gpsimd.memset(blank.rearrange("p (k n) -> p k n", n=2)[:, :, 1], SKIP).then_inc(pool_consts, 1)
            nc.gpsimd.memset(ones[:, :], 1.0).then_inc(pool_consts, 1)
            nc.gpsimd.memset(ident[:, :], 0.0).then_inc(pool_consts, 1)
            nc.gpsimd.memset(eps[:, :], EPS).then_inc(pool_consts, 1)
            nc.gpsimd.iota(riota_i[:, :], [[1, R]], base=0, channel_multiplier=0).then_inc(pool_consts, 1)
            nc.gpsimd.iota(iota_i[:, :], [[1, P]], base=0, channel_multiplier=0).then_inc(pool_consts, 1)
            nc.gpsimd.iota(e1_i[:, :], [[1, EC]], base=1, channel_multiplier=EC).then_inc(pool_consts, 1)
            pool.wait_ge(pool_consts, 10)
            nc.gpsimd.affine_select(out=ident[:, :], in_=ident[:, :], compare_op=ALU.not_equal, fill=1.0, base=0,
                                    pattern=[[-1, P]], channel_multiplier=1).then_inc(pool_consts, 1)
            nc.gpsimd.affine_select(out=upper[:, :], in_=ones[:, :], compare_op=ALU.is_gt, fill=0.0, base=0,
                                    pattern=[[1, P]], channel_multiplier=-1).then_inc(pool_consts, 1)
            nc.gpsimd.memset(gathered[:, :, :], 0.0).then_inc(corner_zero, 1)

            def gather(at_list, column, slot, t):
                nc.gpsimd.indirect_dma_start(gathered[:, 2 * slot + t, :], None, x,
                                             bass.IndirectOffsetOnAxis(ap=at_list[:, column:column + 1], axis=0),
                                             bounds_check=N - 1, oob_is_err=False).then_inc(rows_gathered[slot], 16)

            pool.wait_ge(corner_zero, 1)
            pool.wait_ge(places_ready, 1)
            pool.wait_ge(table_blank, 16)

            def write_columns(i):
                for half in range(2):
                    at_stage = slice(half * SORT_PER, (half + 1) * SORT_PER)
                    if not isinstance(i, int):
                        pool.wait_ge(columns_written[half], 16 * SORT_PER * i)
                        past(pool, pool_past)
                    c = i * (2 * SORT_PER) + half * SORT_PER
                    nc.gpsimd.tensor_copy(place_stage[:, at_stage], place_i[:, bass.ds(c, SORT_PER)]).then_inc(columns_staged, 1)
                    nc.gpsimd.tensor_copy(entry_stage[:, at_stage, :], entries[:, bass.ds(c, SORT_PER), :]).then_inc(columns_staged, 1)
                    pool.wait_ge(columns_staged, 4 * i + 2 * half + 2)
                    if not isinstance(i, int):
                        past(pool, pool_past)
                    for k in range(half * SORT_PER, (half + 1) * SORT_PER):
                        nc.gpsimd.indirect_dma_start(grouped, bass.IndirectOffsetOnAxis(ap=place_stage[:, k:k + 1], axis=0),
                                                     entry_stage[:, k, :], None,
                                                     bounds_check=P * MTP - 1, oob_is_err=False).then_inc(columns_written[half], 16)

            write_columns(0)
            with pool.Fori(1, EC // (2 * SORT_PER)) as i:
                write_columns(i)
            for half in range(2):
                pool.wait_ge(columns_written[half], 16 * EC // 2)
            nc.gpsimd.dma_start(list_at.rearrange("p k n -> p (k n)"), grouped.rearrange("(p k) n -> p (k n)", p=P)).then_inc(list_loaded, 16)
            pool.wait_ge(list_loaded, 16)
            nc.gpsimd.tensor_copy(src_stage[:, 8:8 + 2 * ROWS_RING], src_at[:, 0:2 * ROWS_RING]).then_inc(staged, 1)
            pool.wait_ge(staged, 1)
            for c in range(2 * ROWS_RING):
                gather(src_stage, 8 + c, c // 2, c % 2)

            def write_fixes(at_list, column, slot, t):
                nc.gpsimd.indirect_dma_start(out, bass.IndirectOffsetOnAxis(ap=at_list[:, column:column + 1], axis=0),
                                             y_fix[:, slot, t, :], None,
                                             bounds_check=N - 1, oob_is_err=False).then_inc(fix_scattered[slot], 16)

            def stage(p, kind, width, to, of, lead):
                base = p.count(kind) * 2 + lead
                if not p.looped:
                    skipped, width = max(0, -base), min(width, of.shape[1] - base)
                    if skipped >= width:
                        pool.sem_inc(staged, 1)
                        return
                    base, to = base + skipped, to[:, skipped:width]
                    width -= skipped
                nc.gpsimd.tensor_copy(to, of[:, bass.ds(base, width)]).then_inc(staged, 1)

            def wait_stored(blocks, turns=0):
                for i in range(BLOCK_RING):
                    pool.wait_ge(stored[i], 16 * (turns + (blocks + BLOCK_RING - 1 - i) // BLOCK_RING))

            def step(p):
                if p.kind == "m":
                    return
                if p.kind == "g":
                    slot, out_slot = p.fixed("g") % ROWS_RING, p.fixed("g") % 2
                    column = 2 * (p.fixed("g") % 8)
                    if column % 8 == 0:
                        stage(p, "g", 8, src_stage[:, column:column + 8], src_at, 2 * ROWS_RING)
                        stage(p, "g", 8, edge_stage[:, column:column + 8], edge_at, 0)
                        pool.wait_ge(staged, 2 * p.turns("g", 4) + 3)
                        past(pool, pool_past)
                    pool.wait_ge(turned, p.count("mgf") + 1)
                    if p.looped or p.count("g") + ROWS_RING < MPAIRS:
                        past(pool, pool_past)
                        for t in range(2):
                            gather(src_stage, column + t, slot, t)
                    else:
                        f = p.count("g") + ROWS_RING - MPAIRS
                        nc.gpsimd.memset(gathered[0:1, 2 * slot:2 * slot + 2, :], 0.0).then_inc(corner_zero, 1)
                        pool.wait_ge(corner_zero, f + 2)
                        pool.wait_ge(fix_lists_ready, 2)
                        for t in range(2):
                            gather(fix_at, 2 * f + t, slot, t)
                    pool.wait_ge(message_moved, p.count("g") + 1)
                    past(pool, pool_past)
                    for t in range(2):
                        nc.gpsimd.indirect_dma_start(message_rows, bass.IndirectOffsetOnAxis(ap=edge_stage[:, column + t:column + t + 1], axis=0),
                                                     message_out[:, 2 * out_slot + t, :], None,
                                                     bounds_check=MROWS - 1, oob_is_err=False).then_inc(scattered[out_slot], 16)
                    return
                slot = (MPAIRS + p.fixed("f")) % ROWS_RING
                column = 2 * (p.fixed("f") % 8)
                src_list, src_column, out_list, out_column = fix_src_stage, column, fix_out_stage, column
                if p.at == len(phases) - 1:
                    src_list, src_column = fix_at, 2 * (p.count("f") + ROWS_RING)
                    out_list, out_column = fix_at, 2 * (p.count("f") - BEHIND)
                elif column % 8 == 0:
                    if p.looped or p.count("f") > FIX_RING:
                        pool.wait_ge(moved, nth(p, "f", -1).count("mf") + 1)
                        past(pool, pool_past)
                    stage(p, "f", 8, fix_src_stage[:, column:column + 8], fix_at, 2 * ROWS_RING)
                    stage(p, "f", 8, fix_out_stage[:, column:column + 8], fix_at, -2 * BEHIND)
                    pool.wait_ge(staged, (MPAIRS + 3) // 4 * 2 + 2 * p.turns("f", 4) + 3)
                    past(pool, pool_past)
                if p.looped or p.count("f") + ROWS_RING < FPAIRS:
                    pool.wait_ge(turned, p.count("mgf") + 1)
                    past(pool, pool_past)
                    for t in range(2):
                        gather(src_list, src_column + t, slot, t)
                if p.looped or 0 <= p.count("f") - BEHIND < EARLY:
                    behind = nth(p, "f", -BEHIND)
                    pool.wait_ge(normed, behind.count("mf") + 1)
                    blocks = written(FIX_FROM + p.fixed("f"))
                    wait_stored(blocks, p.s * (p.phase.kinds.count("m") // 2 // BLOCK_RING) if p.looped else 0)
                    past(pool, pool_past)
                    for t in range(2):
                        write_fixes(out_list, out_column + t, behind.fixed("f") % FIX_RING, t)

            walk(pool, phases, step)
            end = Pair(phases, len(phases) - 1, 0, phases[-1].size - 1)
            for f in range(FPAIRS - BEHIND, FPAIRS):
                if f < EARLY:
                    wait_stored(written(MAIN))
                elif f == max(EARLY, FPAIRS - BEHIND):
                    wait_stored(BLOCKS + 1)
                    pool.wait_ge(rest_stored, 16)
                pool.wait_ge(normed, (end if f == FPAIRS - 1 else nth(end, "f", f + 1 - FPAIRS)).count("mf") + 1)
                for t in range(2):
                    write_fixes(fix_at, 2 * f + t, f % FIX_RING, t)
            for i in range(FIX_RING):
                pool.wait_ge(fix_scattered[i], 32 * ((FPAIRS + FIX_RING - 1 - i) // FIX_RING))

            with pool.If(needs_repair(pool)):
                pool.sem_inc(repair_open, 1)
                with pool.Fori(0, FTP) as i:
                    pool.wait_ge(rows_ready, i + 1)
                    past(pool, pool_past)
                    nc.gpsimd.indirect_dma_start(gathered[:, 0, :], None, x, bass.IndirectOffsetOnAxis(ap=rows_i[:, 0:1], axis=0),
                                                 bounds_check=N - 1, oob_is_err=False).then_inc(repair_gathered, 16)
                    pool.wait_ge(repair_result, i + 1)
                    past(pool, pool_past)
                    nc.gpsimd.indirect_dma_start(out, bass.IndirectOffsetOnAxis(ap=rows_i[:, 0:1], axis=0), repair_y, None,
                                                 bounds_check=N - 1, oob_is_err=False).then_inc(repair_written, 16)
                    pool.wait_ge(repair_written, 16 * i + 16)
                    pool.sem_inc(repair_done, 1)

        @block.vector
        def _(dve):
            steps = [0]

            def link(ins):
                steps[0] += 1
                ins.then_inc(dve_step, 1)
                dve.wait_ge(dve_step, steps[0])

            nc.vector.memset(rel_i[:, :], R).then_inc(dve_consts, 1)
            nc.vector.memset(src_i[:, :], 0).then_inc(dve_consts, 1)
            nc.vector.memset(prior[:, :], 0.0).then_inc(dve_consts, 1)
            dve.wait_ge(pool_consts, 12)
            dve.wait_ge(dve_consts, 3)
            link(nc.vector.tensor_copy(riota[:, :], riota_i[:, :]))
            link(nc.vector.tensor_copy(iota_f[:, :], iota_i[:, :]))
            link(nc.vector.tensor_copy(e1_f[:, :], e1_i[:, :]))
            link(nc.vector.tensor_scalar(dead[:, :], e1_f[:, :], E + 0.5, float(SKIP), ALU.is_gt, ALU.mult))
            link(nc.vector.tensor_copy(entries[:, :, 1], e1_i[:, :]))
            dve.wait_ge(edges_in, 64)
            link(nc.vector.tensor_copy(rel_f[:, :], rel_i[:, :]))
            link(nc.vector.tensor_copy(entries[:, :, 0], src_i[:, :]))
            oh = onehot.rearrange("p (r c) -> p r c", r=R)
            rn = running.rearrange("p (r c) -> p r c", r=R)
            pl = placed.rearrange("p (r c) -> p r c", r=R)
            link(nc.vector.tensor_tensor(oh, rel_f.unsqueeze(1).broadcast_to([P, R, EC]), riota.unsqueeze(2).broadcast_to([P, R, EC]), ALU.is_equal))
            nc.vector.tensor_reduce(count[:, :], oh, AX_X, ALU.add).then_inc(counts_ready, 1)
            link(nc.vector.tensor_tensor_scan(running[:, :], onehot[:, :], onehot[:, :], 0.0, ALU.add, ALU.max))
            link(nc.vector.tensor_copy(prior[:, 1:R], rn[:, 0:R - 1, EC - 1]))
            dve.wait_ge(loop_in, 16)
            link(nc.vector.tensor_scalar(w_main[:, :], loop_raw[:, :], C, None, ALU.mult))
            for k in range(KT):
                d = w_main[:, k * D + k * P:k * D + k * P + P]
                link(nc.vector.tensor_tensor(d, d, ident[:, :], ALU.add))
            link(nc.vector.tensor_copy(w_high[:, :], w_main[:, :]))
            nc.vector.tensor_tensor(w_low[:, :], w_main[:, :], w_high[:, :].bitcast(F32), ALU.subtract).then_inc(w_ready, 1)

            def prepare(k):
                if k == 0:
                    dve.wait_ge(counts_summed, 1)
                    link(nc.vector.tensor_copy(total[:, :], misc_ps[:, R:2 * R]))
                    link(nc.vector.tensor_scalar(tot_f[:, :], total[:, :], float(P - 1), None, ALU.add))
                    link(nc.vector.tensor_copy(tot_i[:, :], tot_f[:, :]))
                    link(nc.vector.tensor_scalar(tiles_i[:, :], tot_i[:, :], 7, None, ALU.logical_shift_right))
                    link(nc.vector.tensor_copy(tiles_f[:, :], tiles_i[:, :]))
                    link(nc.vector.tensor_tensor_scan(incl[:, :], tiles_f[:, :], tiles_f[:, :], 0.0, ALU.add, ALU.max))
                    link(nc.vector.tensor_tensor(start[:, :], incl[:, :], tiles_f[:, :], ALU.subtract))
                    link(nc.vector.scalar_tensor_tensor(out=offset[:, :], in0=start[:, :], scalar=float(P), in1=prior[:, :], op0=ALU.mult, op1=ALU.subtract))
                    link(nc.vector.scalar_tensor_tensor(out=count[:, :], in0=offset[:, :], scalar=-1.0, in1=misc_ps[:, 0:R], op0=ALU.add, op1=ALU.add))
                    link(nc.vector.tensor_tensor(pl, rn, count.unsqueeze(2).broadcast_to([P, R, EC]), ALU.add))
                    link(nc.vector.tensor_tensor(rn, pl, oh, ALU.mult))
                    link(nc.vector.tensor_reduce(pos_f[:, :], running.rearrange("p (r c) -> p c r", r=R), AX_X, ALU.add))
                if k == 1:
                    link(nc.vector.tensor_copy(pos_i[:, :], pos_f[:, :]))
                    link(nc.vector.tensor_scalar(hi_i[:, :], pos_i[:, :], 7, None, ALU.logical_shift_right))
                    link(nc.vector.tensor_scalar(lo_i[:, :], pos_i[:, :], P - 1, None, ALU.bitwise_and))
                    link(nc.vector.tensor_copy(hi_f[:, :], hi_i[:, :]))
                    link(nc.vector.tensor_copy(lo_f[:, :], lo_i[:, :]))
                    link(nc.vector.scalar_tensor_tensor(out=place_f[:, :], in0=lo_f[:, :], scalar=float(MTP), in1=hi_f[:, :], op0=ALU.mult, op1=ALU.add))
                    nc.vector.tensor_tensor(place_i[:, :], place_f[:, :], dead[:, :], ALU.add).then_inc(places_ready, 1)
                if k == 3:
                    ge = rel_ge[0:1, :].rearrange("p (k r) -> p k r", r=R - 1)
                    link(nc.vector.tensor_tensor(ge, iota_f[0:1, 0:MTP].unsqueeze(2).broadcast_to([1, MTP, R - 1]),
                                                 start[0:1, 1:R].unsqueeze(1).broadcast_to([1, MTP, R - 1]), ALU.is_ge))
                    link(nc.vector.tensor_reduce(rel_n[0:1, :], ge, AX_X, ALU.add))
                    link(nc.vector.tensor_scalar(w_offset[:, :], rel_n[0:1, :], float(KT * D), None, ALU.mult))

            def prepare_lists(k):
                if k == 0:
                    dve.wait_ge(keys_in, 32)
                    link(nc.vector.tensor_copy(key_f[0:FTP, :], key_i[0:FTP, :]))
                    link(nc.vector.tensor_copy(next_f[0:FTP, :], next_i[0:FTP, :]))
                    link(nc.vector.tensor_tensor(key_eq[0:FTP, :], key_f[0:FTP, :], next_f[0:FTP, :], ALU.is_equal))
                    link(nc.vector.scalar_tensor_tensor(out=key_at[0:FTP, :], in0=key_eq[0:FTP, :], scalar=float(SKIP), in1=key_f[0:FTP, :], op0=ALU.mult, op1=ALU.add))
                    nc.vector.memset(key_at[0:FTP, 0:1], float(SKIP)).then_inc(keys_ready, 1)
                if k == 2:
                    dve.wait_ge(keys_ready, 1)
                    dve.wait_ge(bound_made, 3)
                    link(nc.vector.tensor_tensor(key_eq[0:FTP, :], key_f[0:FTP, :], next_f[0:FTP, :], ALU.is_gt))
                    link(nc.vector.scalar_tensor_tensor(out=key_eq[0:FTP, :], in0=next_f[0:FTP, :], scalar=0.0, in1=key_eq[0:FTP, :],
                                                        op0=ALU.is_ge, op1=ALU.mult))
                    link(nc.vector.tensor_scalar(next_f[0:FTP, :], key_at[0:FTP, :], early_bound[0:FTP, 0:1], None, ALU.is_ge))
                    link(nc.vector.scalar_tensor_tensor(out=next_f[0:FTP, :], in0=key_at[0:FTP, :], scalar=float(N), in1=next_f[0:FTP, :],
                                                        op0=ALU.is_lt, op1=ALU.mult))
                    link(nc.vector.tensor_tensor(next_f[0:FTP, :], next_f[0:FTP, :], key_eq[0:FTP, :], ALU.add))
                    nc.vector.tensor_reduce(disorder[0:FTP, :], next_f[0:FTP, :], AX_X, ALU.add).then_inc(disorder_ready, 1)
                if k == 6:
                    dve.wait_ge(keys_turned, 1)
                    link(nc.vector.tensor_scalar(disorder[:, :], misc_ps[:, 384:385], 0.5, float(SKIP), ALU.is_gt, ALU.mult))
                    nc.vector.tensor_copy(repair_flag[:, :], disorder[0:1, :]).then_inc(flag_ready, 1)
                    nc.vector.tensor_copy(row_key[:, :], misc_ps[:, 128:128 + FTP]).then_inc(fix_lists_ready, 1)
                    nc.vector.tensor_scalar(fix_at[:, :], misc_ps[:, 256:256 + FTP], disorder[:, 0:1], None, ALU.add).then_inc(fix_lists_ready, 1)
                    dve.wait_ge(fix_lists_ready, 2)

            def low(p):
                if p is None or p.plain:
                    return
                slot = p.fixed("mgf") % Y_RING
                dve.wait_ge(copied, p.count("mgf") + 1)
                nc.vector.tensor_tensor(xt_low[:, slot, :], xt_ps[slot % XT_RING][:, :], xt_high[:, slot, :].bitcast(F32), ALU.subtract).then_inc(low_done, 1)

            def same_keys(p):
                if p is None or p.kind != "f":
                    return
                slot, unit_slot = p.fixed("f") % 4, (p.fixed("f") // 4) % 2
                if slot == 0:
                    dve.wait_ge(keys_filled, p.turns("f", 4) + 1)
                user = nth(p, "f", -4)
                if user is not None:
                    dve.wait_ge(product, user.count("mgf") + 1)
                for t in range(2):
                    key = row_key[:, bass.ds(p.count("f") * 2 + t, 1)]
                    nc.vector.tensor_scalar(same[:, 2 * slot + t, :], keys[:, unit_slot, 2 * slot + t, :], key, None, ALU.is_equal).then_inc(same_built, 1)

            def reciprocals(p):
                if p is None or p.kind == "g":
                    return
                g, slot, half = ln_group(p)
                if half == 0:
                    return
                dve.wait_ge(std_ready, g + 1)
                wait(dve, normed, (g - 3) * 2)
                nc.vector.reciprocal(rstd[:, slot, :], std[:, slot, :]).then_inc(rstd_ready, 1)

            def shifts(p):
                if p is None or p.kind == "g":
                    return
                g, slot, half = ln_group(p)
                if half == 0:
                    return
                dve.wait_ge(rstd_ready, g + 1)
                nc.vector.scalar_tensor_tensor(out=shift[:, slot, :], in0=mean_var[:, slot, :, 0], scalar=-1.0, in1=rstd[:, slot, :],
                                               op0=ALU.mult, op1=ALU.mult).then_inc(scale_ready, 1)

            def aggregate(p):
                if p is None or p.kind == "g":
                    return
                g, slot, half = ln_group(p)
                dve.wait_ge(stats_done, p.count("mf") * 2 + 2)
                past(dve, dve_past)
                for t in range(2):
                    nc.vector.bn_aggr(mean_var[:, slot, 2 * half + t, :], stats[:, slot, 2 * half + t, :]).then_inc(moments, 1)

            first_pair = Pair(phases, 0, 0, 0)
            low(first_pair)
            low(first_pair.ahead(1))

            def step(p):
                low(p.ahead(2))
                prepare(sort_step(p))
                prepare_lists(list_step(p))
                part = split_part(p, 16)
                if part is not None:
                    dve.wait_ge(rel_high, part // PART + 1)
                    nc.vector.tensor_tensor(w_rel_low[:, part:part + PART], w_rel[:, part:part + PART],
                                            w_rel_high[:, part:part + PART].bitcast(F32), ALU.subtract).then_inc(rel_split, 1)
                same_keys(p.ahead(3))
                if sort_step(p) == 0:
                    dve.wait_ge(weights_in, 32)
                if p.kind != "g":
                    g, slot, half = ln_group(p)
                    q = p.fixed("mgf") % Y_RING
                    dve.wait_ge(product, p.count("mgf") + 1)
                    if p.kind == "m" and p.fixed("m") % 2 == 0:
                        m = p.fixed("m") // 2
                        wait(dve, stored[m % BLOCK_RING], 16 * p.turns("m", 2 * BLOCK_RING))
                    if p.kind == "f":
                        wait(dve, fix_scattered[p.fixed("f") % FIX_RING], 32 * p.turns("f", FIX_RING))
                    bias_2 = bias_b[:, :].unsqueeze(1).broadcast_to([P, 2, D])
                    if p.kind == "m":
                        m = p.fixed("m")
                        to = y_out[:, (m // 2) % BLOCK_RING, 2 * (m % 2):2 * (m % 2) + 2, :]
                        nc.vector.tensor_tensor(to, y_ps[q][:, :].rearrange("p (t d) -> p t d", t=2), bias_2, ALU.add).then_inc(moved, 1)
                    else:
                        dve.wait_ge(carried, p.count("f") * 2 + (2 if has_carry(p, 1) else 1))
                        for t in range(2):
                            last = nc.vector.tensor_tensor(y_tile(p, t), product_tile(p, t), bias_b[:, :], ALU.add)
                        last.then_inc(moved, 1)
                reciprocals(p.ahead(-2))
                aggregate(p.ahead(-1))
                shifts(p.ahead(-2))
                if p.kind != "g":
                    n = p.count("mf")
                    dve.wait_ge(moved, n + 1)
                    past(dve, dve_past)
                    for t in range(2):
                        nc.vector.bn_stats(stats[:, slot, 2 * half + t, :], y_tile(p, t)).then_inc(stats_done, 1)
            walk(dve, phases, step)
            end = Pair(phases, len(phases) - 1, phases[-1].n - 1, phases[-1].size - 1)
            aggregate(end)
            reciprocals(end)
            shifts(end)

            with dve.If(needs_repair(dve)):
                dve.wait_ge(repair_open, 1)
                nc.vector.tensor_copy(edge_key[:, :], row_key[:, :]).then_inc(edge_key_ready, 1)
                dve.wait_ge(edge_key_ready, 1)
                nc.vector.memset(edge_key[0:1, :], -3.0).then_inc(edge_key_ready, 1)
                dve.wait_ge(edge_key_ready, 2)
                dve.sem_inc(own_keys_used, 1)
                dve.sem_inc(repair_done, 1)
                with dve.Fori(0, FTP) as i:
                    def then(ins, k):
                        ins.then_inc(repair_chain, 1)
                        dve.wait_ge(repair_chain, i * 9 + k)
                        past(dve, dve_past)

                    key = row_key[:, bass.ds(i, 1)]
                    dve.wait_ge(own_keys_loaded, 16 * i + 16)
                    dve.wait_ge(repair_done, i + 1)
                    past(dve, dve_past)
                    then(nc.vector.tensor_scalar(later[:, :], own_keys[:, :], key, None, ALU.is_equal), 1)
                    then(nc.vector.tensor_tensor(later[:, :], later[:, :], upper[:, :], ALU.mult), 2)
                    then(nc.vector.tensor_reduce(later_n[:, :], later[:, :], AX_X, ALU.add), 3)
                    then(nc.vector.tensor_scalar(rows_f[:, :], key, 0.0, None, ALU.is_lt), 4)
                    then(nc.vector.tensor_tensor(later_n[:, :], later_n[:, :], rows_f[:, :], ALU.add), 5)
                    then(nc.vector.scalar_tensor_tensor(out=rows_f[:, :], in0=later_n[:, :], scalar=float(SKIP), in1=key, op0=ALU.mult, op1=ALU.add), 6)
                    then(nc.vector.memset(rows_f[0:1, :], float(SKIP)), 7)
                    nc.vector.tensor_copy(rows_i[:, :], rows_f[:, :]).then_inc(rows_ready, 1)
                    with dve.Fori(0, CHUNKS // 2) as c:
                        for half in range(2):
                            dve.wait_ge(chunk_used, i * CHUNKS + c * 2 + half + 1)
                            past(dve, dve_past)
                            for k in range(WINDOWS):
                                last = nc.vector.tensor_scalar(masks[half][:, k, :], own_keys[:, :], edge_key[:, bass.ds((c * 2 + half) * WINDOWS + k, 1)], None, ALU.is_equal)
                            last.then_inc(masks_built, 1)
                    dve.wait_ge(masks_built, i * CHUNKS + CHUNKS)
                    dve.sem_inc(own_keys_used, 1)
                    dve.wait_ge(repair_product, i + 1)
                    past(dve, dve_past)
                    then(nc.vector.tensor_tensor(repair_y, y_ps[0][:, 0:D], bias_b[:, :], ALU.add), 8)
                    then(nc.vector.bn_stats(stats[:, 0, 0, :], repair_y), 9)
                    nc.vector.bn_aggr(mean_var[:, 0, 0, :], stats[:, 0, 0, :]).then_inc(repair_var, 1)
                    dve.wait_ge(repair_std, i + 1)
                    past(dve, dve_past)
                    nc.vector.reciprocal(rstd[:, 0, 0:1], std[:, 0, 0:1]).then_inc(repair_scale, 1)
                    dve.wait_ge(repair_scale, 2 * i + 1)
                    past(dve, dve_past)
                    nc.vector.scalar_tensor_tensor(out=shift[:, 0, 0:1], in0=mean_var[:, 0, 0, 0:1], scalar=-1.0, in1=rstd[:, 0, 0:1],
                                                   op0=ALU.mult, op1=ALU.mult).then_inc(repair_scale, 1)

        @block.scalar
        def _(act):
            def copy_xt(p):
                if p is None:
                    return
                n, slot = p.count("mgf"), p.fixed("mgf") % Y_RING
                act.wait_ge(turned, n + 1)
                wait(act, product, n - Y_RING + 1)
                to = xt_full if p.plain else xt_high
                nc.scalar.activation(to[:, slot, :], xt_ps[slot % XT_RING][:, :], ACT.Copy).then_inc(copied, 1)

            def carry(p, t):
                if p is None or p.kind != "f":
                    return
                if not has_carry(p, t):
                    return
                nxt = p if t == 0 else nth(p, "f", 1)
                slot = nxt.fixed("f") % 4
                act.wait_ge(message_loaded[slot], 32 * (nxt.turns("f", 4) + 1))
                if t == 0:
                    act.wait_ge(tile_sum, p.count("f") + 1)
                else:
                    act.wait_ge(product, p.count("mgf") + 1)
                nc.scalar.activation(message_in[0:1, 2 * slot + 1 - t, :], product_tile(p, t)[0:1, :], ACT.Copy).then_inc(carried, 1)

            def fill_keys(p):
                if p is None or p.kind != "f" or p.fixed("f") % 4:
                    return
                slot = (p.fixed("f") // 4) % 2
                act.wait_ge(keys_loaded[slot], 16 * (p.turns("f", 8) + 1))
                nc.scalar.activation(keys[:, slot, :, 0], keys[:, slot, :, RUN], ACT.Copy).then_inc(keys_filled, 1)

            def move_message(p):
                if p is None or p.kind != "g":
                    return
                q, slot = p.fixed("mgf") % Y_RING, p.fixed("g") % 2
                act.wait_ge(product, p.count("mgf") + 1)
                wait(act, scattered[slot], 32 * p.turns("g", 2))
                nc.scalar.activation(message_out[:, 2 * slot:2 * slot + 2, :], y_ps[q][:, :].rearrange("p (t d) -> p t d", t=2),
                                     ACT.Copy, scale=C).then_inc(message_moved, 1)

            def deviation(p):
                if p is None or p.kind == "g":
                    return
                g, slot, half = ln_group(p)
                if half == 0:
                    return
                act.wait_ge(moments, (g + 1) * 4)
                nc.scalar.activation(std[:, slot, :], mean_var[:, slot, :, 1], ACT.Sqrt, bias=eps[:, 0:1]).then_inc(std_ready, 1)

            def norm(p, t):
                if p.kind == "g":
                    return
                g, slot, half = ln_group(p)
                if t == 0:
                    act.wait_ge(scale_ready, g + 1)
                i = 2 * half + t
                a = nc.scalar.activation(y_tile(p, t), y_tile(p, t), ACT.Identity, scale=rstd[:, slot, i:i + 1], bias=shift[:, slot, i:i + 1])
                if t == 1:
                    a.then_inc(normed, 1)

            act.wait_ge(pool_consts, 12)
            first_pair = Pair(phases, 0, 0, 0)
            for d in range(6):
                copy_xt(first_pair.ahead(d))
            for d in range(2):
                deviation(first_pair.ahead(d))

            def step(p):
                carry(p.ahead(4), 0)
                copy_xt(p.ahead(6))
                part = split_part(p, 0)
                if part is not None:
                    act.wait_ge(weights_in, 32)
                    nc.scalar.activation(w_rel_high[:, part:part + PART], w_rel[:, part:part + PART], ACT.Copy).then_inc(rel_high, 1)
                deviation(p.ahead(2))
                norm(p, 0)
                carry(p.ahead(4), 1)
                move_message(p.ahead(4))
                norm(p, 1)
                fill_keys(p.ahead(10))

            walk(act, phases, step)

            with act.If(needs_repair(act)):
                act.wait_ge(repair_open, 1)
                with act.Fori(0, FTP) as i:
                    act.wait_ge(repair_turned, i + 1)
                    past(act, act_past)
                    nc.scalar.activation(xt_full[:, 0, 0:D], xt_ps[0][:, 0:D], ACT.Copy).then_inc(repair_copied, 1)
                    act.wait_ge(repair_var, i + 1)
                    past(act, act_past)
                    nc.scalar.activation(std[:, 0, 0:1], mean_var[:, 0, 0, 1:2], ACT.Sqrt, bias=eps[:, 0:1]).then_inc(repair_std, 1)
                    act.wait_ge(repair_scale, 2 * i + 2)
                    past(act, act_past)
                    nc.scalar.activation(repair_y, repair_y, ACT.Identity, scale=rstd[:, 0, 0:1], bias=shift[:, 0, 0:1]).then_inc(repair_result, 1)

        @block.tensor
        def _(pe):
            def turn(p):
                if p is None:
                    return
                n, q = p.count("mgf"), p.fixed("mgf")
                if p.kind == "m":
                    m = p.fixed("m")
                    slot = (m // 2) % BLOCK_RING
                    if m % 2 == 0:
                        pe.wait_ge(x_loaded[slot], 16 * (p.turns("m", 2 * BLOCK_RING) + 1))
                    elif not p.looped and p.count("m") == MAIN - 1:
                        pe.wait_ge(x_rest_loaded, 16)
                    rows = [x_in[:, slot, 2 * (m % 2) + t, :] for t in range(2)]
                else:
                    gf = p.fixed("gf")
                    pe.wait_ge(rows_gathered[gf % ROWS_RING], 32 * (p.turns("gf", ROWS_RING) + 1))
                    rows = [gathered[:, 2 * (gf % ROWS_RING) + t, :] for t in range(2)]
                before = p.ahead(-1)
                if before is not None:
                    wait(pe, copied, n - 1)
                    wait(pe, low_done, before.splits())
                for t in range(2):
                    for k in range(KT):
                        last = nc.tensor.transpose(xt_ps[q % XT_RING][:, t * D + k * P:t * D + (k + 1) * P], rows[t][:, k * P:(k + 1) * P], ident[:, :])
                last.then_inc(turned, 1)

            def multiply(p, offsets):
                n, q = p.count("mgf"), p.fixed("mgf") % Y_RING
                pe.wait_ge(copied, n + 1)
                if p.at == mix_at + 1 and not p.looped and p.s == 0 and p.j == 0:
                    pe.wait_ge(rel_split, 8)
                if not p.plain:
                    pe.wait_ge(low_done, p.splits() + 1)
                for d in (Y_RING, 2):
                    user = p.ahead(-d)
                    if user is None or (d == 2 and "f" not in (p.kind, user.kind)):
                        continue
                    if user.kind == "g":
                        pe.wait_ge(message_moved, user.count("g") + 1)
                    else:
                        pe.wait_ge(moved, user.count("mf") + 1)
                for t in range(2):
                    to = product_tile(p, t)

                    def part(xt, w, k, start, stop):
                        return nc.tensor.matmul(to, xt[:, q, t * D + k * P:t * D + (k + 1) * P], w, start=start, stop=stop)

                    for k in range(KT):
                        ws = slice(k * D, (k + 1) * D)
                        whole, high, low = w_main, w_high, w_low
                        if p.kind == "g":
                            whole, high, low = w_rel, w_rel_high, w_rel_low
                            ws = bass.ds(offsets[t] + k * D, D)
                        end = k == KT - 1 and p.kind != "f"
                        if p.plain:
                            last = part(xt_full, whole[:, ws], k, k == 0, end)
                        else:
                            part(xt_high, low[:, ws], k, k == 0, False)
                            part(xt_low, high[:, ws], k, False, False)
                            last = part(xt_high, high[:, ws], k, False, end)
                    if p.kind == "f":
                        f = p.count("f")
                        slot = p.fixed("f") % 4
                        if t == 0:
                            pe.wait_ge(message_loaded[slot], 32 * (p.turns("f", 4) + 1))
                            pe.wait_ge(same_built, f * 2 + 2)
                        wait(pe, carried, f * 2 + t)
                        last = nc.tensor.matmul(to, same[:, 2 * slot + t, :], message_in[:, 2 * slot + t, :], start=False, stop=True)
                        if t == 0:
                            last.then_inc(tile_sum, 1)
                last.then_inc(product, 1)

            pe.wait_ge(pool_consts, 12)

            first_pair = Pair(phases, 0, 0, 0)
            turn(first_pair)
            turn(first_pair.ahead(1))
            pe.wait_ge(counts_ready, 1)
            nc.tensor.matmul(misc_ps[:, 0:R], upper[:, :], count[:, :], start=True, stop=True)
            nc.tensor.matmul(misc_ps[:, R:2 * R], ones[:, :], count[:, :], start=True, stop=True).then_inc(counts_summed, 1)
            pe.wait_ge(w_ready, 1)

            def step(p):
                offsets = None
                if p.kind == "g":
                    n = p.count("g") * 2
                    offsets = [pe.value_load(w_offset[0:1, bass.ds(n + t, 1)], min_val=0, max_val=(R - 1) * KT * D) for t in range(2)]
                turn(p.ahead(2))
                multiply(p, offsets)
                if list_step(p) == 4:
                    pe.wait_ge(keys_ready, 1)
                    nc.tensor.transpose(misc_ps[:, 128:128 + FTP], key_f[0:FTP, :], ident[0:FTP, 0:FTP])
                    nc.tensor.transpose(misc_ps[:, 256:256 + FTP], key_at[0:FTP, :], ident[0:FTP, 0:FTP])
                    pe.wait_ge(disorder_ready, 1)
                    nc.tensor.matmul(misc_ps[:, 384:385], ones[0:FTP, :], disorder[0:FTP, :], start=True, stop=True).then_inc(keys_turned, 1)
            walk(pe, phases, step)

            with pe.If(needs_repair(pe)):
                pe.wait_ge(repair_open, 1)
                pe.sem_inc(chunk_used, 2)
                with pe.Fori(0, FTP) as i:
                    pe.wait_ge(repair_gathered, 16 * i + 16)
                    past(pe, pe_past)
                    for k in range(KT):
                        last = nc.tensor.transpose(xt_ps[0][:, k * P:(k + 1) * P], gathered[:, 0, k * P:(k + 1) * P], ident[:, :])
                    last.then_inc(repair_turned, 1)
                    pe.wait_ge(repair_copied, i + 1)
                    past(pe, pe_past)
                    to = y_ps[0][:, 0:D]
                    for k in range(KT):
                        nc.tensor.matmul(to, xt_full[:, 0, k * P:(k + 1) * P], w_main[:, k * D:(k + 1) * D], start=k == 0, stop=False)
                    with pe.Fori(0, CHUNKS // 2) as c:
                        for half in range(2):
                            pe.wait_ge(masks_built, i * CHUNKS + c * 2 + half + 1)
                            pe.wait_ge(chunk_loaded[half], (i * (CHUNKS // 2) + c + 1) * 16)
                            past(pe, pe_past)
                            for k in range(WINDOWS):
                                last = nc.tensor.matmul(to, masks[half][:, k, :], message_chunk[half][:, k, :], start=False, stop=False)
                            last.then_inc(chunk_used, 1)
                    nc.tensor.matmul(to, zero[:, 0:P], zero[:, 0:D], start=False, stop=True).then_inc(repair_product, 1)


_INS = ["x", "src", "dst", "edge_type_8", "L0_gnn_weight", "L0_gnn_h_bias", "L0_gnn_loop_weight"]


def kernel(**inputs):
    import concourse.bacc as bacc
    from concourse.bass_utils import run_bass_kernel_spmd

    nc = bacc.Bacc("TRN2", target_bir_lowering=False, num_devices=1)
    arrays, args = {}, []
    for name in _INS:
        a = np.ascontiguousarray(inputs[name])
        arrays[f"in_{name}"] = a
        args.append(nc.dram_tensor(f"in_{name}", a.shape, mybir.dt.from_np(a.dtype), kind="ExternalInput").ap())
    args.append(nc.dram_tensor("out_rows", inputs["x"].shape, F32, kind="ExternalOutput").ap())
    gnn_layernorm_kernel(nc, *args)
    r = run_bass_kernel_spmd(nc, [arrays], core_ids=[0])
    return r.results[0]["out_rows"]
```
